# Optimizing a Trainium2 kernel written in Bass

```python
import numpy as np
import jax
import jax.numpy as jnp

def _softmax(x, axis=-1):
    return jax.nn.softmax(x, axis=axis)

def _gelu(x):
    return jax.nn.gelu(x, approximate=True)

def _silu(x):
    return jax.nn.silu(x)

def _sigmoid(x):
    return jax.nn.sigmoid(x)

def _layernorm(x, axis=-1, eps=1e-05):
    m = jnp.mean(x, axis=axis, keepdims=True)
    v = jnp.var(x, axis=axis, keepdims=True)
    return (x - m) / jnp.sqrt(v + eps)

def _scatter_add(tgt, idx, src, axis=0):
    return tgt.at[idx].add(src)

def _segment_sum(src, seg, n):
    return jax.ops.segment_sum(src, seg, n)
kernel_name = 'mk_xattn_ffn_d1_seqx_r4_b9a22c'

def setup_inputs(seed: int=0):
    np.random.seed(seed)
    _w = jnp.asarray

    def _rec_inputs():
        import jax
        import jax.numpy as jnp
        _rk = jax.random.key(seed)
        x = 7.22e-05 + 1 * jax.random.normal(jax.random.fold_in(_rk, 1), (4, 512, 512), jnp.float32)
        _lenS = 512 - jax.random.randint(jax.random.fold_in(_rk, 7), (4,), 0, max(1, 512 // 4) + 1, jnp.int32)
        _lenS2 = 512 - jax.random.randint(jax.random.fold_in(_rk, 8), (4,), 0, max(1, 512 // 4) + 1, jnp.int32)
        _ctx_1024P = jax.random.normal(jax.random.fold_in(_rk, 11), (4, 16, 256), jnp.float32)
        _ctx_1024c = jax.random.dirichlet(jax.random.fold_in(_rk, 511), 0.3 * jnp.ones((16,), jnp.float32), (4, 512))
        _ctx_1024t = jnp.einsum('bsk,bkd->bsd', _ctx_1024c, _ctx_1024P)
        _ctx_1024t = _ctx_1024t * jax.lax.rsqrt(jnp.mean(jnp.square(_ctx_1024t)) + 1e-12) * 0.953939
        ctx_1024 = -0.000673644 + 1.00013 * (_ctx_1024t + 0.3 * jax.random.normal(jax.random.fold_in(_rk, 611), (4, 512, 256), jnp.float32))
        return (x, ctx_1024)
    x, ctx_1024 = _rec_inputs()

    def _L0_xattn_setup():
        import jax, jax.numpy as jnp
        import numpy as np
        B, S1, S2, DCA = (2, 512, 256, 16)
        QDIM, KDIM, H = (512, 256, 16)
        HD = QDIM // H
        SCALE = HD ** (-0.5)
        EPS = 1e-06
        DCA_WEIGHT = 1.0

        def _ln(t, w, b):
            m = jnp.mean(t, axis=-1, keepdims=True)
            v = jnp.var(t, axis=-1, keepdims=True)
            return (t - m) * jax.lax.rsqrt(v + EPS) * w + b

        def _attn(q, k, v):
            s = jnp.einsum('bhqd,bhkd->bhqk', q, k) * SCALE
            p = jax.nn.softmax(s, axis=-1)
            return jnp.einsum('bhqk,bhkd->bhqd', p, v)
        key = jax.random.key(seed)
        ks = jax.random.split(key, 8)
        w = lambda k, shape: jax.random.normal(k, shape, jnp.float32) * 0.02
        return {'x': jax.random.normal(ks[0], (B, S1, QDIM), jnp.float32), 'y': jax.random.normal(ks[1], (B, S2 + DCA, KDIM), jnp.float32), 'Wq': w(ks[2], (QDIM, QDIM)), 'bq': jnp.zeros((QDIM,), jnp.float32), 'Wk': w(ks[3], (KDIM, QDIM)), 'bk': jnp.zeros((QDIM,), jnp.float32), 'Wv': w(ks[4], (KDIM, QDIM)), 'bv': jnp.zeros((QDIM,), jnp.float32), 'Wkv_dca': w(ks[5], (KDIM, 2 * QDIM)), 'bkv_dca': jnp.zeros((2 * QDIM,), jnp.float32), 'qn_w': jnp.ones((HD,), jnp.float32), 'qn_b': jnp.zeros((HD,), jnp.float32), 'kn_w': jnp.ones((HD,), jnp.float32), 'kn_b': jnp.zeros((HD,), jnp.float32), 'kn_dca_w': jnp.ones((HD,), jnp.float32), 'kn_dca_b': jnp.zeros((HD,), jnp.float32), 'Wo': w(ks[6], (QDIM, QDIM)), 'bo': jnp.zeros((QDIM,), jnp.float32)}
    _L0_xattn_all = _L0_xattn_setup()
    _L0_xattn_in = {k: v for k, v in _L0_xattn_all.items() if k in ('Wq', 'bq', 'Wk', 'bk', 'Wv', 'bv', 'Wkv_dca', 'bkv_dca', 'qn_w', 'qn_b', 'kn_w', 'kn_b', 'kn_dca_w', 'kn_dca_b', 'Wo', 'bo')}
    del _L0_xattn_all

    def _L0_ffn_setup():
        import jax, jax.numpy as jnp
        import numpy as np
        HIDDEN = 512
        INTER = 1376
        LUT_SIZE = 16

        def _ghost_linear(x, idx, lut):
            w = lut[idx]
            return jnp.einsum('bsh,oh->bso', x, w)
        key = jax.random.key(seed)
        k_x, k_lut, k_g, k_u, k_d = jax.random.split(key, 5)
        x = jax.random.normal(k_x, (2, 1024, HIDDEN), dtype=jnp.float32)
        lut = jax.random.normal(k_lut, (LUT_SIZE,), dtype=jnp.float32) * 0.02
        gate_idx = jax.random.randint(k_g, (INTER, HIDDEN), 0, LUT_SIZE, dtype=jnp.int32)
        up_idx = jax.random.randint(k_u, (INTER, HIDDEN), 0, LUT_SIZE, dtype=jnp.int32)
        down_idx = jax.random.randint(k_d, (HIDDEN, INTER), 0, LUT_SIZE, dtype=jnp.int32)
        return {'x': x, 'lut': lut, 'gate_idx': gate_idx, 'up_idx': up_idx, 'down_idx': down_idx}
    _L0_ffn_all = _L0_ffn_setup()
    _L0_ffn_in = {k: v for k, v in _L0_ffn_all.items() if k in ('lut', 'gate_idx', 'up_idx', 'down_idx')}
    del _L0_ffn_all
    return {'x': x, 'ctx_1024': ctx_1024, 'L0_xattn_Wq': _L0_xattn_in['Wq'], 'L0_xattn_bq': _L0_xattn_in['bq'], 'L0_xattn_Wk': _L0_xattn_in['Wk'], 'L0_xattn_bk': _L0_xattn_in['bk'], 'L0_xattn_Wv': _L0_xattn_in['Wv'], 'L0_xattn_bv': _L0_xattn_in['bv'], 'L0_xattn_Wkv_dca': _L0_xattn_in['Wkv_dca'], 'L0_xattn_bkv_dca': _L0_xattn_in['bkv_dca'], 'L0_xattn_qn_w': _L0_xattn_in['qn_w'], 'L0_xattn_qn_b': _L0_xattn_in['qn_b'], 'L0_xattn_kn_w': _L0_xattn_in['kn_w'], 'L0_xattn_kn_b': _L0_xattn_in['kn_b'], 'L0_xattn_kn_dca_w': _L0_xattn_in['kn_dca_w'], 'L0_xattn_kn_dca_b': _L0_xattn_in['kn_dca_b'], 'L0_xattn_Wo': _L0_xattn_in['Wo'], 'L0_xattn_bo': _L0_xattn_in['bo'], 'L0_ffn_lut': _L0_ffn_in['lut'], 'L0_ffn_gate_idx': _L0_ffn_in['gate_idx'], 'L0_ffn_up_idx': _L0_ffn_in['up_idx'], 'L0_ffn_down_idx': _L0_ffn_in['down_idx']}

def reference(x, ctx_1024, L0_xattn_Wq, L0_xattn_bq, L0_xattn_Wk, L0_xattn_bk, L0_xattn_Wv, L0_xattn_bv, L0_xattn_Wkv_dca, L0_xattn_bkv_dca, L0_xattn_qn_w, L0_xattn_qn_b, L0_xattn_kn_w, L0_xattn_kn_b, L0_xattn_kn_dca_w, L0_xattn_kn_dca_b, L0_xattn_Wo, L0_xattn_bo, L0_ffn_lut, L0_ffn_gate_idx, L0_ffn_up_idx, L0_ffn_down_idx):
    import jax
    import jax.numpy as jnp

    def _L0_xattn_ref(x, y, Wq, bq, Wk, bk, Wv, bv, Wkv_dca, bkv_dca, qn_w, qn_b, kn_w, kn_b, kn_dca_w, kn_dca_b, Wo, bo):
        import jax, jax.numpy as jnp
        import numpy as np
        B, S1, S2, DCA = (2, 512, 256, 16)
        QDIM, KDIM, H = (512, 256, 16)
        HD = QDIM // H
        SCALE = HD ** (-0.5)
        EPS = 1e-06
        DCA_WEIGHT = 1.0

        def _ln(t, w, b):
            m = jnp.mean(t, axis=-1, keepdims=True)
            v = jnp.var(t, axis=-1, keepdims=True)
            return (t - m) * jax.lax.rsqrt(v + EPS) * w + b

        def _attn(q, k, v):
            s = jnp.einsum('bhqd,bhkd->bhqk', q, k) * SCALE
            p = jax.nn.softmax(s, axis=-1)
            return jnp.einsum('bhqk,bhkd->bhqd', p, v)
        b, s1, _ = x.shape
        y_dca = y[:, -DCA:, :]
        y_main = y[:, :-DCA, :]
        kv_dca = (y_dca @ Wkv_dca + bkv_dca).reshape(b, DCA, 2, H, HD)
        k_dca = _ln(kv_dca[:, :, 0], kn_dca_w, kn_dca_b)
        v_dca = kv_dca[:, :, 1]
        s2 = y_main.shape[1]
        q = _ln((x @ Wq + bq).reshape(b, s1, H, HD), qn_w, qn_b)
        kv = jnp.concatenate([y_main @ Wk + bk, y_main @ Wv + bv], axis=-1)
        kv = kv.reshape(b, s2, H, 2 * HD)
        k = _ln(kv[..., :HD], kn_w, kn_b)
        v = kv[..., HD:]
        qT = q.transpose(0, 2, 1, 3)
        ctx = _attn(qT, k.transpose(0, 2, 1, 3), v.transpose(0, 2, 1, 3))
        ctx = ctx.transpose(0, 2, 1, 3).reshape(b, s1, QDIM)
        ctx_dca = _attn(qT, k_dca.transpose(0, 2, 1, 3), v_dca.transpose(0, 2, 1, 3))
        ctx_dca = ctx_dca.transpose(0, 2, 1, 3).reshape(b, s1, QDIM)
        ctx = ctx + DCA_WEIGHT * ctx_dca
        return ctx @ Wo + bo

    def _L0_ffn_ref(x, lut, gate_idx, up_idx, down_idx):
        import jax, jax.numpy as jnp
        import numpy as np
        HIDDEN = 512
        INTER = 1376
        LUT_SIZE = 16

        def _ghost_linear(x, idx, lut):
            w = lut[idx]
            return jnp.einsum('bsh,oh->bso', x, w)
        gate = _ghost_linear(x, gate_idx, lut)
        up = _ghost_linear(x, up_idx, lut)
        h = jax.nn.silu(gate) * up
        return _ghost_linear(h, down_idx, lut)
    x = x + _L0_xattn_ref(_layernorm(x, axis=-1), ctx_1024, L0_xattn_Wq, L0_xattn_bq, L0_xattn_Wk, L0_xattn_bk, L0_xattn_Wv, L0_xattn_bv, L0_xattn_Wkv_dca, L0_xattn_bkv_dca, L0_xattn_qn_w, L0_xattn_qn_b, L0_xattn_kn_w, L0_xattn_kn_b, L0_xattn_kn_dca_w, L0_xattn_kn_dca_b, L0_xattn_Wo, L0_xattn_bo)
    x = x + _L0_ffn_ref(_layernorm(x, axis=-1), L0_ffn_lut, L0_ffn_gate_idx, L0_ffn_up_idx, L0_ffn_down_idx)
    return x

_drawn_inputs = setup_inputs


def setup_inputs(seed=0):
    import zlib

    import numpy as np

    out = dict(_drawn_inputs(seed))
    spreads = {'L0_xattn_bq': (0.0, 0.698),
     'L0_xattn_bk': (0.0, 0.1),
     'L0_xattn_bv': (0.0, 0.1),
     'L0_xattn_bkv_dca': (0.0, 0.1),
     'L0_xattn_qn_w': (1.0, 0.6),
     'L0_xattn_qn_b': (0.0, 0.8),
     'L0_xattn_kn_w': (1.0, 0.6),
     'L0_xattn_kn_b': (0.0, 0.8),
     'L0_xattn_kn_dca_w': (1.0, 0.6),
     'L0_xattn_kn_dca_b': (0.0, 0.8),
     'L0_xattn_bo': (0.0, 0.1)}
    factors = {}
    for name, (base, spread) in spreads.items():
        noise = np.random.default_rng([zlib.crc32(name.encode()), seed]).standard_normal(out[name].shape)
        drawn = base * np.exp(spread * noise) if base else spread * noise
        out[name] = jnp.asarray(drawn.astype(out[name].dtype))
    for name, factor in factors.items():
        out[name] = (out[name] * factor).astype(out[name].dtype)
    return out
```

```python
from contextlib import ExitStack

import concourse.bass as bass
from concourse import mybir

F32 = mybir.dt.float32
F16 = mybir.dt.float16
I32 = mybir.dt.int32
U16 = mybir.dt.uint16
ALU = mybir.AluOpType
ACT = mybir.ActivationFunctionType
AX_X = mybir.AxisListType.X

P = 128
B, S, D = 4, 512, 512
KD = 256
H, HD = 16, 32
DCA = 16
INTER = 1376
NLUT = 16
T = S // P
KQ, KC = D // P, KD // P
G = H * HD // P
HG = P // HD
IT = -(-INTER // P)
LAST = INTER - (IT - 1) * P
WCOLS = 2 * KQ * INTER + IT * D
CH = 520
NCH = WCOLS // CH
QK_SCALE = float(HD) ** -0.5
WS = 256.0
EPS_X, EPS_H = 1e-5, 1e-6
UP0, DN0 = KQ * INTER, 2 * KQ * INTER
HALF = H // 2
assert NCH * CH == WCOLS and NCH % 2 == 0


def xattn_ffn(nc, A, out):
    nc.disable_value_cache = True
    ctx = ExitStack()
    with ctx:
        def sb(name, shape, dt):
            return ctx.enter_context(nc.sbuf_tensor(name, shape, dt))

        def sem(name):
            return ctx.enter_context(nc.semaphore(name))

        wf_hi = sb("wf_hi", [P, WCOLS], F16)
        wf_lo = sb("wf_lo", [P, WCOLS], F16)
        wq = [sb(f"wq{i}", [P, KQ, D], F16) for i in range(2)]
        wk = [sb(f"wk{i}", [P, KC, D], F16) for i in range(2)]
        wv = [sb(f"wv{i}", [P, KC, D], F16) for i in range(2)]
        wd = [sb(f"wd{i}", [P, KC, 2 * D], F16) for i in range(2)]
        wo = [sb(f"wo{i}", [P, G, D], F16) for i in range(2)]
        bq, bk, bdk, bo = (sb(n, [P, D], F32) for n in ("bq", "bk", "bdk", "bo"))
        bvm, bvd, bvs = (sb(n, [P, G], F32) for n in ("bvm", "bvd", "bvs"))
        lnw = {n: sb("ln_" + n, [P, HD], F32) for n in ("qw", "qb", "kw", "kb", "kw0", "kb0")}
        ident = sb("ident", [P, P], F32)
        ident_h = sb("ident_h", [P, P], F16)
        lut = sb("lut", [P, NLUT], F32)
        lut_d = sb("lut_d", [P, NLUT // 2], F32)
        mhalf = sb("mhalf", [P, H], F32)
        cmean = sb("cmean", [P, 64], F32)
        idle = sb("idle", [P, 2], F32)
        stat = sb("stat", [P, 2, 6], F32)
        mv = sb("mv", [P, 2, 2], F32)
        xvar = sb("xvar", [P, 2], F32)
        xrstd = sb("xrstd", [P, 2], F32)
        hvar = sb("hvar", [P, 2, H], F32)
        hrstd = sb("hrstd", [P, 2, H], F32)
        nmax = sb("nmax", [P, 2, T, H], F32)
        den = sb("den", [P, 2, T, H], F32)
        lnden = sb("lnden", [P, 2, T, H], F32)
        shift = sb("shift", [P, 2, T, H], F32)
        caug = sb("caug", [P, T, H, 2, 2], F16)

        NA = 23552
        arena = sb("arena", [P, NA], F32)
        at = [0]

        def cut(words):
            a = at[0]
            at[0] += words
            assert at[0] <= NA, at[0]
            return arena[:, a:a + words]

        x_sb = cut(T * D).rearrange("p (t n) -> p t n", t=T)
        xT = [cut(KQ * S // 2).bitcast(F16).rearrange("p (k s) -> p k s", k=KQ) for _ in range(2)]
        cT = [cut(KC * S // 2).bitcast(F16).rearrange("p (k s) -> p k s", k=KC) for _ in range(2)]
        blk = [cut(H * 96 // 2).bitcast(F16).rearrange("p (h c) -> p h c", h=H) for _ in range(2)]
        qv0 = at[0]
        qT = cut(H * S // 2).bitcast(F16).rearrange("p (h s) -> p h s", h=H)
        v_sb = cut(T * D).rearrange("p (t n) -> p t n", t=T)
        hT = [arena[:, qv0 + i * IT * S // 2:qv0 + (i + 1) * IT * S // 2].bitcast(F16)
              .rearrange("p (i s) -> p i s", i=IT) for i in range(2)]
        assert IT * S <= at[0] - qv0
        kT = cut(H * S // 2).bitcast(F16).rearrange("p (h s) -> p h s", h=H)
        p0 = at[0]
        probs = [cut(HG * S).rearrange("p (j s) -> p j s", j=HG) for _ in range(2)]
        ctx_raw = arena[:, p0:p0 + KC * S]
        sd = arena[:, p0:p0 + T * H * DCA].rearrange("p (r k) -> p r k", k=DCA)
        qc = [cut(D) for _ in range(2)]
        qn = [cut(D) for _ in range(2)]
        sq = cut(D)
        aT = xT
        used = at[0]

        at[0] = 0
        l_w = [cut(CH) for _ in range(2)]
        l_idx = [cut(CH).bitcast(I32) for _ in range(2)]
        l_b0 = [cut(CH).bitcast(I32) for _ in range(2)]
        l_f = cut(CH // 2).bitcast(F16)
        l_m = [cut(CH // 2).bitcast(U16) for _ in range(7)]
        l_leaf = [[cut(CH) for _ in range(7)] for _ in range(2)]
        st_q = cut(KQ * D)
        st_kv = [cut(KC * D) for _ in range(2)]
        st_d = cut(KC * 2 * D)
        st_o = cut(G * D)
        pat = [cut(HALF * HD // 2).bitcast(F16).rearrange("p (h c) -> p h c", h=HALF) for _ in range(2)]

        pS = [ctx.enter_context(nc.psum_tensor(f"pS{i}", [P, 2, 512], F32)) for i in range(2)]
        pJ = [ctx.enter_context(nc.psum_tensor(f"pJ{i}", [P, 512], F32)) for i in range(2)]
        pT = [ctx.enter_context(nc.psum_tensor(f"pT{i}", [P, 512], F32)) for i in range(2)]
        pTh = [t[:, :].bitcast(F16).rearrange("p (h s) -> p h s", h=HALF) for t in pT]

        names = """wq_in wkv_in wd_in wo_in small_in kw0_in lut_in idx_in0 idx_in1
            ident_set pat_set pat_ps pat_copied pool_chain dve_chain w_hi w_cent w_lo lut_ready
            b0_set leaf_act leaf_pool l_selected l_hi l_lo
            x_in ctx_in out_stored
            xvar_set xrstd_set xn_set xT_ps xT_hi xT_lo cT_hi cT_lo xb_set
            proj_done proj_evac v_evac sq_set var_set hrstd_set qn_set blk_hi blk_set blk_ps blk_act blk_dve
            S_done max_set S_exp sd_set ed_set den_set ln_set c_set aug_ps aug_act aug_dve
            ST_done probs_set pv_done aT_hi aT_lo wo_done x2_set
            gu_done silu_set h_set h_hi h_lo down_done y_set""".split()
        s = {n: sem(n) for n in names}

        NXN, NPROJ, NPE, NU, NS, NG, NIT = 2 * T, 2 * T + 2 + T, 2 * T + 1, 2 * T, T * H // 2, G, IT
        NX2 = 2 * T

        block = ctx.enter_context(nc.Block())

        @block.sync
        def _(sp):
            sp.dma_start(st_q.rearrange("p (k n) -> p k n", k=KQ),
                         A["Wq"].rearrange("(k p) n -> p k n", p=P)).then_inc(s["wq_in"], 16)
            for i, n in enumerate(("Wk", "Wv")):
                sp.dma_start(st_kv[i].rearrange("p (k n) -> p k n", k=KC),
                             A[n].rearrange("(k p) n -> p k n", p=P)).then_inc(s["wkv_in"], 16)
            sp.dma_start(st_d.rearrange("p (k n) -> p k n", k=KC),
                         A["Wkv_dca"].rearrange("(k p) n -> p k n", p=P)).then_inc(s["wd_in"], 16)
            sp.dma_start(st_o.rearrange("p (k n) -> p k n", k=G),
                         A["Wo"].rearrange("(k p) n -> p k n", p=P)).then_inc(s["wo_in"], 16)
            def lookup_pair(c, first):
                for i in range(2):
                    done, col = (0, i * CH) if first else (sp.snap(c * 2), sp.snap(c * (2 * CH) + i * CH))
                    if not first:
                        sp.wait_ge(s["l_selected"], done)
                    sp.dma_start(l_idx[i], A["idx"][:, bass.ds(col, CH)]).then_inc(s[f"idx_in{i}"], 16)

            lookup_pair(0, True)
            with sp.Fori(1, NCH // 2) as c:
                lookup_pair(c, False)
            sp.wait_ge(s["l_lo"], NCH)
            sp.wait_ge(s["w_lo"], 5)
            sp.wait_ge(s["pat_copied"], 2 * T)
            def batch(b, rows, first):
                if not first:
                    sp.wait_ge(s["out_stored"], sp.snap(b * (16 * T)))
                sp.dma_start(x_sb, A["x"][bass.ds(b, 1)].rearrange("a (t p) n -> p (a t) n", p=P)).then_inc(s["x_in"], 16)
                sp.dma_start(ctx_raw.rearrange("p (k n) -> p k n", k=KC),
                             A["ctxT"][bass.ds(b, 1)].rearrange("a (k p) n -> p (a k) n", p=P)).then_inc(s["ctx_in"], 16)
                for t in range(T):
                    sp.wait_ge(s["y_set"], b * T + t + 1 if first else sp.snap(b * T + t + 1))
                    sp.dma_start(out.rearrange("b s n -> (b s n)")[bass.ds(rows[t], P * D)].rearrange("(p n) -> p n", n=D),
                                 x_sb[:, t, :]).then_inc(s["out_stored"], 16)

            batch(0, [t * (P * D) for t in range(T)], True)
            with sp.Fori(1, B) as b:
                batch(b, [sp.snap(b * (S * D) + t * (P * D)) for t in range(T)], False)
            sp.wait_ge(s["out_stored"], 16 * T * B)

        @block.gpsimd
        def _(pool):
            n = [0]

            def take_wait():
                pool.tensor_tensor(idle[:, 0:1], mhalf[:, 0:1], mhalf[:, 0:1], ALU.mult)

            def link(ins):
                n[0] += 1
                ins.then_inc(s["pool_chain"], 1)
                pool.wait_ge(s["pool_chain"], n[0])

            def row(name, lo, hi):
                a = A[name][lo:hi]
                return a.rearrange("(o n) -> o n", o=1)

            for dst, src in ((bq, row("bq", 0, D)), (bk, row("bk", 0, D)), (bo, row("bo", 0, D)), (bdk, row("bkv_dca", 0, D))):
                pool.dma_start(dst[:, :], src.to_broadcast([P, D])).then_inc(s["small_in"], 16)
            pool.dma_start(bvm[:, :], A["bv"]).then_inc(s["small_in"], 16)
            pool.dma_start(bvd[:, :], A["bvd"]).then_inc(s["small_in"], 16)
            for key, name in (("qw", "qn_w"), ("qb", "qn_b"), ("kw", "kn_w"), ("kb", "kn_b")):
                pool.dma_start(lnw[key][:, :], row(name, 0, HD).to_broadcast([P, HD])).then_inc(s["small_in"], 16)
            for key, name in (("kw0", "kn_w"), ("kb0", "kn_b")):
                pool.dma_start(lnw[key][DCA:P, :], row(name, 0, HD).to_broadcast([P - DCA, HD])).then_inc(s["small_in"], 16)
            for key, name in (("kw0", "kn_dca_w"), ("kb0", "kn_dca_b")):
                pool.dma_start(lnw[key][0:DCA, :], row(name, 0, HD).to_broadcast([DCA, HD])).then_inc(s["small_in"], 16)
            pool.dma_start(lut[:, :], row("lut", 0, NLUT).to_broadcast([P, NLUT])).then_inc(s["lut_in"], 16)

            link(pool.memset(ident[:, :], 0.0))
            pool.affine_select(out=ident[:, :], in_=ident[:, :], compare_op=ALU.not_equal, fill=1.0, base=0,
                               pattern=[[-1, P]], channel_multiplier=1).then_inc(s["ident_set"], 1)
            link(pool.memset(ident_h[:, :], 0.0))
            pool.affine_select(out=ident_h[:, :], in_=ident_h[:, :], compare_op=ALU.not_equal, fill=1.0, base=0,
                               pattern=[[-1, P]], channel_multiplier=1).then_inc(s["ident_set"], 1)
            pool.memset(mhalf[:, :], -0.5).then_inc(s["ident_set"], 1)
            link(pool.memset(pat[0][:, :, :], 0.0))
            link(pool.memset(pat[1][:, :, :], 0.0))
            for j in range(HALF):
                for i in range(2):
                    link(pool.memset(pat[i][:, j, 4 * j:4 * j + 2], 1.0))
                link(pool.memset(pat[0][0:DCA, j, 4 * j:4 * j + 2], 0.0))
                link(pool.memset(pat[0][0:DCA, j, 4 * j + 2:4 * j + 4], 1.0))
            pool.memset(cmean[:, 0:1], 0.0).then_inc(s["pat_set"], 1)

            pool.wait_ge(s["lut_ready"], 2)
            def lookup_pair(c, first):
                for i in range(2):
                    pool.wait_ge(s["b0_set"], c * 2 + i + 1)
                    if not first:
                        pool.wait_ge(s["l_selected"], c * 2)
                        take_wait()
                    for j in range(4, 8):
                        last = pool.tensor_scalar(l_leaf[i][j - 1], l_b0[i], lut_d[:, j:j + 1], lut[:, 2 * j:2 * j + 1],
                                                  ALU.mult, ALU.add)
                    last.then_inc(s["leaf_pool"], 1)

            lookup_pair(0, True)
            with pool.Fori(1, NCH // 2) as c:
                lookup_pair(c, False)
            base = n[0]
            with pool.Fori(0, B) as b:
                k = [0]
                PER = 2 * 2 * T

                def chain(ins):
                    k[0] += 1
                    ins.then_inc(s["pool_chain"], 1)
                    pool.wait_ge(s["pool_chain"], b * PER + (base + k[0]))

                def ln_rstd(n_):
                    pool.wait_ge(s["xvar_set"], b * NX2 + n_ + 1)
                    pool.tensor_tensor(xrstd[:, n_ % 2:n_ % 2 + 1], xvar[:, n_ % 2:n_ % 2 + 1], mhalf[:, 0:1],
                                       ALU.pow).then_inc(s["xrstd_set"], 1)

                for t in range(T):
                    ln_rstd(t)
                for t in range(T):
                    pool.wait_ge(s["xn_set"], b * NX2 + t + 1)
                    pool.tensor_tensor(x_sb[:, t, :], x_sb[:, t, :], bo[:, :], ALU.add).then_inc(s["xb_set"], 1)
                for u in range(NU):
                    w, bb = ((lnw["qw"], lnw["qb"]) if u < T else (lnw["kw0"], lnw["kb0"]) if u == T
                             else (lnw["kw"], lnw["kb"]))
                    v3 = lambda a: a.rearrange("p (h d) -> p h d", d=HD)
                    i = u % 2
                    pool.wait_ge(s["var_set"], b * NU + u + 1)
                    if u >= 2:
                        pool.wait_ge(s["blk_set"], b * NU + u - 1)
                    pool.tensor_tensor(hrstd[:, i, :], hvar[:, i, :], mhalf[:, :], ALU.pow).then_inc(s["hrstd_set"], 1)
                    pool.wait_ge(s["hrstd_set"], b * NU + u + 1)
                    chain(pool.tensor_tensor(v3(qn[i]), v3(qc[i]), hrstd[:, i, :].unsqueeze(2).to_broadcast([P, H, HD]), ALU.mult))
                    chain(pool.tensor_tensor(v3(qn[i]), v3(qn[i]), w[:, :].unsqueeze(1).to_broadcast([P, H, HD]), ALU.mult))
                    pool.tensor_tensor(v3(qn[i]), v3(qn[i]), bb[:, :].unsqueeze(1).to_broadcast([P, H, HD]),
                                       ALU.add).then_inc(s["qn_set"], 1)
                for t in range(T):
                    ln_rstd(T + t)
                for it in range(IT):
                    m = P if it < IT - 1 else LAST
                    pool.wait_ge(s["h_set"], b * IT + it + 1)
                    take_wait()
                    pool.tensor_scalar(hT[0][0:m, it, :], qc[it % 2][0:m, :], 1.0, 0.0, ALU.mult, ALU.add).then_inc(s["h_hi"], 1)
                assert k[0] == PER

        @block.scalar
        def _(act):
            act.wait_ge(s["w_cent"], 1)
            act.activation(wq[0][:, :, :].rearrange("p k n -> p (k n)"), st_q, ACT.Copy, scale=WS).then_inc(s["w_hi"], 1)
            act.wait_ge(s["w_cent"], 2)
            act.activation(wk[0][:, :, :].rearrange("p k n -> p (k n)"), st_kv[0], ACT.Copy, scale=WS)
            act.activation(wv[0][:, :, :].rearrange("p k n -> p (k n)"), st_kv[1], ACT.Copy, scale=WS).then_inc(s["w_hi"], 1)
            act.wait_ge(s["w_cent"], 3)
            act.activation(wd[0][:, :, :].rearrange("p k n -> p (k n)"), st_d, ACT.Copy, scale=WS).then_inc(s["w_hi"], 1)
            act.wait_ge(s["wo_in"], 16)
            act.activation(wo[0][:, :, :].rearrange("p k n -> p (k n)"), st_o, ACT.Copy, scale=WS).then_inc(s["w_hi"], 1)

            act.wait_ge(s["lut_ready"], 2)
            def lookup_pair(c, first):
                for i in range(2):
                    act.wait_ge(s["b0_set"], c * 2 + i + 1)
                    if not first:
                        act.wait_ge(s["l_lo"], c * 2)
                    for j in range(4):
                        last = act.activation(l_w[i] if j == 0 else l_leaf[i][j - 1], l_b0[i], ACT.Identity,
                                              scale=lut_d[:, j:j + 1], bias=lut[:, 2 * j:2 * j + 1])
                    last.then_inc(s["leaf_act"], 1)
                    act.wait_ge(s["l_selected"], c * 2 + i + 1)
                    act.activation(wf_hi[:, bass.ds(c * (2 * CH) + i * CH, CH)], l_w[i], ACT.Copy).then_inc(s["l_hi"], 1)

            lookup_pair(0, True)
            with act.Fori(1, NCH // 2) as c:
                lookup_pair(c, False)
            for t in range(T):
                act.wait_ge(s["pat_ps"], 2)
                act.wait_ge(s["l_lo"], NCH)
                for half in range(2):
                    act.activation(kT[96:P, half * HALF:(half + 1) * HALF, t * P:(t + 1) * P],
                                   pTh[min(t, 1)][96:P, :, :], ACT.Copy).then_inc(s["pat_copied"], 1)

            with act.Fori(0, B) as b:
                def x_hi(n_):
                    t = n_ % T
                    act.wait_ge(s["xT_ps"], b * NX2 + n_ + 1)
                    act.activation(xT[0][:, :, t * P:(t + 1) * P], pT[n_ % 2][:, :].rearrange("p (k s) -> p k s", k=KQ),
                                   ACT.Copy).then_inc(s["xT_hi"], 1)

                act.wait_ge(s["ctx_in"], b * 16 + 16)
                act.activation(cT[0].rearrange("p k s -> p (k s)"), ctx_raw, ACT.Copy).then_inc(s["cT_hi"], 1)
                for t in range(T):
                    x_hi(t)

                def square(u):
                    ev = u + 1 if u < T else u + 2
                    act.wait_ge(s["proj_evac"], b * (NU + 1) + ev)
                    if u:
                        act.wait_ge(s["var_set"], b * NU + u)
                    act.activation(sq, qc[u % 2], ACT.Square).then_inc(s["sq_set"], 1)

                def values(t):
                    if t == 0:
                        act.wait_ge(s["proj_done"], b * NPROJ + T + 3)
                        act.activation(v_sb[:, 0, :], pJ[0][:, :], ACT.Copy, scale=1.0 / WS).then_inc(s["v_evac"], 1)
                        act.wait_ge(s["proj_done"], b * NPROJ + T + 4)
                        act.wait_ge(s["v_evac"], b * (T + 1) + 1)
                        act.activation(v_sb[0:DCA, 0, :], pJ[1][0:DCA, :], ACT.Copy, scale=1.0 / WS).then_inc(s["v_evac"], 1)
                    else:
                        act.wait_ge(s["proj_done"], b * NPROJ + T + 4 + 2 * t)
                        act.activation(v_sb[:, t, :], pJ[1][:, :], ACT.Copy, scale=1.0 / WS).then_inc(s["v_evac"], 1)

                def block_hi(u):
                    act.wait_ge(s["qn_set"], b * NU + u + 1)
                    if u >= 2:
                        act.wait_ge(s["blk_ps"], b * (2 * NU) + 2 * (u - 1))
                    src = qn[u % 2].rearrange("p (h d) -> p h d", d=HD)
                    o = blk[u % 2]
                    act.activation(o[:, :, 0:HD], src, ACT.Copy)
                    second = HD if u < T else 2 * HD
                    act.activation(o[:, :, second:second + HD], src, ACT.Copy).then_inc(s["blk_hi"], 1)

                def block_out(u):
                    act.wait_ge(s["blk_ps"], b * (2 * NU) + 2 * u + 1)
                    dst = qT if u < T else kT
                    t = u % T
                    act.activation(dst[0:96, 0:HALF, t * P:(t + 1) * P], pTh[0][0:96, :, :], ACT.Copy).then_inc(s["blk_act"], 1)

                for u in range(NU + 2):
                    if u < NU:
                        square(u)
                        if u >= T:
                            values(u - T)
                    if 1 <= u <= NU:
                        block_hi(u - 1)
                    if u >= 2:
                        block_out(u - 2)

                for m in range(NS):
                    t, p = divmod(m, H // 2)
                    act.wait_ge(s["S_done"], b * NS + m + 1)
                    act.wait_ge(s["max_set"], b * NS + m + 1)
                    for j in range(2):
                        h = 2 * p + j
                        last = act.activation(pS[m % 2][:, j, DCA:S], pS[m % 2][:, j, DCA:S], ACT.Exp,
                                              bias=nmax[:, 0, t, h:h + 1], accum_out=den[:, 0, t, h:h + 1])
                    last.then_inc(s["S_exp"], 1)
                act.wait_ge(s["sd_set"], b + 1)
                sdf = sd.rearrange("p r k -> p (r k)")
                act.activation(sdf, sdf, ACT.Exp).then_inc(s["ed_set"], 1)
                act.wait_ge(s["den_set"], b + 1)
                act.wait_ge(s["S_exp"], (b + 1) * NS)
                act.activation(lnden[:, :, :, :].rearrange("p a t h -> p (a t h)"),
                               den[:, :, :, :].rearrange("p a t h -> p (a t h)"), ACT.Ln).then_inc(s["ln_set"], 1)
                act.wait_ge(s["aug_ps"], b + 1)
                act.activation(qT[96:P, 0:HALF, :], pT[0][96:P, :].bitcast(F16)[:, 0:S].unsqueeze(1).to_broadcast([32, HALF, S]),
                               ACT.Copy).then_inc(s["aug_act"], 1)

                def attn_hi(g):
                    act.wait_ge(s["pv_done"], b * (G * T) + T * (g + 1))
                    act.activation(aT[0][:, g, :], pJ[g % 2][:, :], ACT.Identity, bias=bvs[:, g:g + 1]).then_inc(s["aT_hi"], 1)

                for n_ in range(G * T):
                    for p in range(2):
                        r = 2 * n_ + p
                        act.wait_ge(s["ST_done"], b * (2 * G * T) + r + 1)
                        if p == 0 and n_ >= 2:
                            act.wait_ge(s["pv_done"], b * (G * T) + n_ - 1)
                        act.activation(probs[n_ % 2][:, 2 * p:2 * p + 2, :], pS[r % 2][:, :, :], ACT.Exp).then_inc(s["probs_set"], 1)
                    if n_ % T == 1 and n_ > T:
                        attn_hi(n_ // T - 1)
                attn_hi(G - 1)

                for t in range(T):
                    x_hi(T + t)
                for it in range(IT):
                    m = P if it < IT - 1 else LAST
                    act.wait_ge(s["gu_done"], b * IT + it + 1)
                    if it >= 2:
                        act.wait_ge(s["h_set"], b * IT + it - 1)
                    act.activation(qn[it % 2][0:m, :], pS[it % 2][0:m, 0, :], ACT.Silu, scale=1.0 / WS).then_inc(s["silu_set"], 1)

        @block.vector
        def _(dve):
            n = [0]

            def take_wait():
                dve.memset(idle[:, 1:2], 0.0)

            def link(ins):
                n[0] += 1
                ins.then_inc(s["dve_chain"], 1)
                dve.wait_ge(s["dve_chain"], n[0])

            def centre(v):
                r = v.shape[1]
                link(dve.tensor_reduce(cmean[:, 0:r], v, AX_X, ALU.add))
                link(dve.tensor_scalar(cmean[:, 0:r], cmean[:, 0:r], 1.0 / HD, None, ALU.mult))
                return dve.tensor_tensor(v, v, cmean[:, 0:r].unsqueeze(2).to_broadcast([P, r, HD]), ALU.subtract)

            heads = lambda a: a.rearrange("p (h d) -> p h d", d=HD)
            dve.wait_ge(s["pat_set"], 1)
            dve.wait_ge(s["lut_in"], 16)
            link(dve.tensor_scalar(lut[:, :], lut[:, :], WS, None, ALU.mult))
            lp = lut[:, :].rearrange("p (j e) -> p j e", e=2)
            dve.tensor_tensor(lut_d[:, :], lp[:, :, 1], lp[:, :, 0], ALU.subtract).then_inc(s["lut_ready"], 2)
            dve.wait_ge(s["wq_in"], 16)
            centre(heads(st_q)).then_inc(s["w_cent"], 1)
            dve.wait_ge(s["wkv_in"], 32)
            dve.wait_ge(s["w_cent"], 1)
            centre(heads(st_kv[0])).then_inc(s["w_cent"], 1)
            dve.wait_ge(s["wd_in"], 16)
            dk = st_d.rearrange("p (k n) -> p k n", k=KC)
            dve.wait_ge(s["w_cent"], 2)
            link(centre(heads(dk[:, 0, 0:D])))
            centre(heads(dk[:, 1, 0:D])).then_inc(s["w_cent"], 1)
            n_small = 4 + 2 + 4 + 2 + 2
            dve.wait_ge(s["small_in"], 16 * n_small)
            dve.wait_ge(s["w_cent"], 3)
            for t_ in (bq, bk, bdk):
                link(centre(heads(t_[:, :])))
            link(dve.tensor_scalar(lnw["qw"][:, :], lnw["qw"][:, :], QK_SCALE, None, ALU.mult))
            link(dve.tensor_scalar(lnw["qb"][:, :], lnw["qb"][:, :], QK_SCALE, None, ALU.mult))
            link(dve.tensor_tensor(bvs[:, :], bvm[:, :], bvd[:, :], ALU.add))
            fl = lambda a: a[:, :, :].rearrange("p k n -> p (k n)")

            def low(dst, src, hi):
                return dve.scalar_tensor_tensor(out=dst, in0=src, scalar=WS, in1=hi, op0=ALU.mult, op1=ALU.subtract)

            dve.wait_ge(s["w_hi"], 1)
            low(fl(wq[1]), st_q, fl(wq[0])).then_inc(s["w_lo"], 1)
            dve.wait_ge(s["w_hi"], 2)
            low(fl(wk[1]), st_kv[0], fl(wk[0])).then_inc(s["w_lo"], 1)
            low(fl(wv[1]), st_kv[1], fl(wv[0])).then_inc(s["w_lo"], 1)
            dve.wait_ge(s["w_hi"], 3)
            low(fl(wd[1]), st_d, fl(wd[0])).then_inc(s["w_lo"], 1)
            dve.wait_ge(s["w_hi"], 4)
            low(fl(wo[1]), st_o, fl(wo[0])).then_inc(s["w_lo"], 1)

            base_l = n[0]
            per_l = 8
            def lookup_pair(c, first):
                for i in range(2):
                    dve.wait_ge(s[f"idx_in{i}"], c * 16 + 16)
                    if not first:
                        dve.wait_ge(s["leaf_act"], c * 2)
                        dve.wait_ge(s["leaf_pool"], c * 2)
                    dve.tensor_scalar(l_b0[i], l_idx[i], 1, None, ALU.bitwise_and).then_inc(s["b0_set"], 1)
                    k0 = i * per_l
                    dve.tensor_scalar(l_f, l_idx[i], 1.0, None, ALU.mult).then_inc(s["dve_chain"], 1)
                    dve.wait_ge(s["dve_chain"], c * (2 * per_l) + (base_l + k0 + 1))
                    def mask(j):
                        return dve.tensor_scalar(l_m[j - 1], l_f, 2.0 * j, None, ALU.is_ge)

                    mask(1)
                    mask(2).then_inc(s["dve_chain"], 1)
                    dve.wait_ge(s["leaf_act"], c * 2 + i + 1)
                    dve.wait_ge(s["dve_chain"], c * (2 * per_l) + (base_l + k0 + 2))
                    for j in range(1, 8):
                        if j == 4:
                            dve.wait_ge(s["leaf_pool"], c * 2 + i + 1)
                        if j + 2 < 8:
                            mask(j + 2)
                        else:
                            take_wait()
                        ins = dve.copy_predicated(l_w[i], l_m[j - 1], l_leaf[i][j - 1])
                        if j < 7:
                            ins.then_inc(s["dve_chain"], 1)
                            dve.wait_ge(s["dve_chain"], c * (2 * per_l) + (base_l + k0 + 2 + j))
                    ins.then_inc(s["l_selected"], 1)
                    dve.wait_ge(s["l_hi"], c * 2 + i + 1)
                    cols = bass.ds(c * (2 * CH) + i * CH, CH)
                    dve.tensor_tensor(wf_lo[:, cols], l_w[i], wf_hi[:, cols], ALU.subtract).then_inc(s["l_lo"], 1)

            lookup_pair(0, True)
            with dve.Fori(1, NCH // 2) as c:
                lookup_pair(c, False)
            base = base_l + NCH * per_l
            PER = 2 * 2 * T + 2 * T + 3
            with dve.Fori(0, B) as b:
                k = [0]

                def chain(ins):
                    k[0] += 1
                    ins.then_inc(s["dve_chain"], 1)
                    dve.wait_ge(s["dve_chain"], b * PER + (base + k[0]))

                def layernorm(n_):
                    t, i = n_ % T, n_ % 2
                    chain(dve.bn_stats(stat[:, i, :], x_sb[:, t, :]))
                    take_wait()
                    chain(dve.bn_aggr(mv[:, i, :], stat[:, i, :]))
                    dve.tensor_scalar(xvar[:, i:i + 1], mv[:, i, 1:2], EPS_X, None, ALU.add).then_inc(s["xvar_set"], 1)
                    dve.wait_ge(s["xrstd_set"], b * NX2 + n_ + 1)
                    if n_ % T >= 2:
                        dve.wait_ge(s["xT_ps"], b * NX2 + n_ - 1)
                    dve.tensor_scalar(qn[i], x_sb[:, t, :], mv[:, i, 0:1], xrstd[:, i:i + 1], ALU.subtract, ALU.mult)\
                       .then_inc(s["xn_set"], 1)

                def x_lo(n_):
                    t = n_ % T
                    dve.wait_ge(s["xT_hi"], b * NX2 + n_ + 1)
                    cols = slice(t * P, (t + 1) * P)
                    dve.tensor_tensor(xT[1][:, :, cols], pT[n_ % 2][:, :].rearrange("p (k s) -> p k s", k=KQ),
                                      xT[0][:, :, cols], ALU.subtract).then_inc(s["xT_lo"], 1)

                dve.wait_ge(s["ctx_in"], b * 16 + 16)
                dve.wait_ge(s["cT_hi"], b + 1)
                fc = lambda a: a.rearrange("p k s -> p (k s)")
                dve.tensor_tensor(fc(cT[1]), ctx_raw, fc(cT[0]), ALU.subtract).then_inc(s["cT_lo"], 1)
                dve.wait_ge(s["x_in"], b * 16 + 16)
                for t in range(T + 1):
                    if t < T:
                        layernorm(t)
                    if t:
                        x_lo(t - 1)

                def project_out(u):
                    q = b * NPROJ
                    dve.wait_ge(s["proj_done"], q + (u + 1 if u <= T else T + 3 + 2 * (u - T)))
                    if u >= 2:
                        dve.wait_ge(s["qn_set"], b * NU + u - 1)
                    dve.scalar_tensor_tensor(out=qc[u % 2], in0=pJ[0 if u >= T else u % 2][:, :], scalar=1.0 / WS,
                                             in1=(bq if u < T else bk)[:, :], op0=ALU.mult, op1=ALU.add).then_inc(s["proj_evac"], 1)
                    if u == T:
                        dve.wait_ge(s["proj_done"], q + T + 2)
                        dve.wait_ge(s["proj_evac"], b * (NU + 1) + T + 1)
                        dve.scalar_tensor_tensor(out=qc[u % 2][0:DCA], in0=pJ[1][0:DCA, :], scalar=1.0 / WS,
                                                 in1=bdk[0:DCA, :], op0=ALU.mult, op1=ALU.add).then_inc(s["proj_evac"], 1)

                def variance(u):
                    i = u % 2
                    dve.wait_ge(s["sq_set"], b * NU + u + 1)
                    chain(dve.tensor_reduce(hvar[:, i, :], heads(sq), AX_X, ALU.add))
                    dve.tensor_scalar(hvar[:, i, :], hvar[:, i, :], 1.0 / HD, EPS_H, ALU.mult, ALU.add).then_inc(s["var_set"], 1)

                def block_lo(u):
                    dve.wait_ge(s["blk_hi"], b * NU + u + 1)
                    o = blk[u % 2]
                    c0 = 2 * HD if u < T else HD
                    dve.tensor_tensor(o[:, :, c0:c0 + HD], heads(qn[u % 2]), o[:, :, 0:HD], ALU.subtract).then_inc(s["blk_set"], 1)

                def block_out(u):
                    dve.wait_ge(s["blk_ps"], b * (2 * NU) + 2 * u + 2)
                    dst = qT if u < T else kT
                    t = u % T
                    dve.tensor_copy(dst[0:96, HALF:H, t * P:(t + 1) * P], pTh[1][0:96, :, :]).then_inc(s["blk_dve"], 1)

                for u in range(NU + 2):
                    if u < NU:
                        project_out(u)
                        variance(u)
                    if 1 <= u <= NU:
                        block_lo(u - 1)
                    if u >= 2:
                        block_out(u - 2)

                for m in range(NS):
                    t, p = divmod(m, H // 2)
                    dve.wait_ge(s["S_done"], b * NS + m + 1)
                    dve.tensor_reduce(nmax[:, 0, t, 2 * p:2 * p + 2], pS[m % 2][:, :, DCA:S], AX_X, ALU.max,
                                      negate=True)
                    dve.tensor_copy(sd[:, t * H + 2 * p:t * H + 2 * p + 2, :], pS[m % 2][:, :, 0:DCA]).then_inc(s["max_set"], 1)
                dve.wait_ge(s["max_set"], (b + 1) * NS)
                nm1 = nmax[:, 1, :, :].rearrange("p t h -> p (t h)")
                chain(dve.tensor_reduce(nm1, sd, AX_X, ALU.max, negate=True))
                dve.tensor_tensor(sd, sd, nm1.unsqueeze(2).to_broadcast([P, T * H, DCA]), ALU.add).then_inc(s["sd_set"], 1)
                dve.wait_ge(s["ed_set"], b + 1)
                dve.tensor_reduce(den[:, 1, :, :].rearrange("p t h -> p (t h)"), sd, AX_X, ALU.add).then_inc(s["den_set"], 1)
                dve.wait_ge(s["ln_set"], b + 1)
                fs = lambda a: a[:, :, :, :].rearrange("p a t h -> p (a t h)")
                chain(dve.tensor_tensor(fs(shift), fs(nmax), fs(lnden), ALU.subtract))
                for w in range(2):
                    dst = caug[:, :, :, w, 0]
                    ins = dve.tensor_copy(dst, shift[:, w, :, :])
                chain(ins)
                for w in range(2):
                    last = dve.tensor_tensor(caug[:, :, :, w, 1], shift[:, w, :, :], caug[:, :, :, w, 0], ALU.subtract)
                last.then_inc(s["c_set"], 1)
                dve.wait_ge(s["aug_ps"], b + 1)
                dve.wait_ge(s["aug_act"], b + 1)
                dve.tensor_copy(qT[96:P, HALF:H, :], pT[0][96:P, :].bitcast(F16)[:, S:2 * S].unsqueeze(1).to_broadcast([32, HALF, S]))\
                   .then_inc(s["aug_dve"], 1)

                for g in range(G):
                    dve.wait_ge(s["aT_hi"], b * G + g + 1)
                    dve.scalar_tensor_tensor(out=aT[1][:, g, :], in0=pJ[g % 2][:, :], scalar=bvs[:, g:g + 1], in1=aT[0][:, g, :],
                                             op0=ALU.add, op1=ALU.subtract).then_inc(s["aT_lo"], 1)
                for t in range(T):
                    dve.wait_ge(s["wo_done"], b * T + t + 1)
                    dve.wait_ge(s["xb_set"], b * T + t + 1)
                    dve.scalar_tensor_tensor(out=x_sb[:, t, :], in0=pJ[t % 2][:, :], scalar=1.0 / WS, in1=x_sb[:, t, :],
                                             op0=ALU.mult, op1=ALU.add).then_inc(s["x2_set"], 1)
                for t in range(T + 1):
                    if t < T:
                        dve.wait_ge(s["x2_set"], b * T + t + 1)
                        layernorm(T + t)
                    if t:
                        x_lo(T + t - 1)

                for it in range(IT):
                    m = P if it < IT - 1 else LAST
                    dve.wait_ge(s["silu_set"], b * IT + it + 1)
                    dve.scalar_tensor_tensor(out=qc[it % 2][0:m], in0=pS[it % 2][0:m, 1, :], scalar=1.0 / WS,
                                             in1=qn[it % 2][0:m], op0=ALU.mult, op1=ALU.mult).then_inc(s["h_set"], 1)
                    dve.wait_ge(s["h_hi"], b * IT + it + 1)
                    dve.tensor_tensor(hT[1][0:m, it, :], qc[it % 2][0:m], hT[0][0:m, it, :], ALU.subtract).then_inc(s["h_lo"], 1)
                for t in range(T):
                    dve.wait_ge(s["down_done"], b * T + t + 1)
                    dve.scalar_tensor_tensor(out=x_sb[:, t, :], in0=pJ[t % 2][:, :], scalar=1.0 / WS, in1=x_sb[:, t, :],
                                             op0=ALU.mult, op1=ALU.add).then_inc(s["y_set"], 1)
                assert k[0] == PER, k[0]

        @block.tensor
        def _(pe):
            pe.wait_ge(s["pat_set"], 1)
            pe.wait_ge(s["ident_set"], 3)
            for i in range(2):
                for j in range(HALF):
                    last = pe.transpose(pTh[i][96:P, j, :], pat[i][:, j, :], ident_h[:, :])
                last.then_inc(s["pat_ps"], 1)
            pe.wait_ge(s["pat_copied"], 2 * T)
            pe.wait_ge(s["w_lo"], 5)

            def product(dst, lhs, rhs, k, wait=None):
                for i in range(k):
                    if wait is not None:
                        wait(i)
                    for a, c in ((0, 0), (0, 1), (1, 0)):
                        last = pe.matmul(dst, lhs(a, i), rhs(c, i), start=(i == 0 and a == 0 and c == 0),
                                         stop=(i == k - 1 and a == 1))
                return last

            with pe.Fori(0, B) as b:
                def transpose_x(n_):
                    t, i = n_ % T, n_ % 2
                    pe.wait_ge(s["xn_set"], b * NX2 + n_ + 1)
                    if n_ % T >= 2:
                        pe.wait_ge(s["xT_lo"], b * NX2 + n_ - 1)
                    for k in range(KQ):
                        last = pe.transpose(pT[i][:, k * P:(k + 1) * P], qn[i][:, k * P:(k + 1) * P], ident[:, :])
                    last.then_inc(s["xT_ps"], 1)

                def proj_q(t):
                    pe.wait_ge(s["xT_lo"], b * NX2 + t + 1)
                    if t >= 2:
                        pe.wait_ge(s["proj_evac"], b * (NU + 1) + t - 1)
                    product(pJ[t % 2][:, :], lambda a, i: xT[a][:, i, t * P:(t + 1) * P],
                            lambda c, i: wq[c][:, i, :], KQ).then_inc(s["proj_done"], 1)

                def proj_c(dst, t, w, c0):
                    product(pJ[dst][:, :], lambda a, i: cT[a][:, i, t * P:(t + 1) * P],
                            lambda c, i: w[c][:, i, c0:c0 + D], KC).then_inc(s["proj_done"], 1)

                def proj_kv(t):
                    ev, vv = b * (NU + 1), b * (T + 1)
                    if t == 0:
                        pe.wait_ge(s["cT_lo"], b + 1)
                        pe.wait_ge(s["proj_evac"], ev + T - 1)
                        proj_c(0, 0, wk, 0)
                        pe.wait_ge(s["proj_evac"], ev + T)
                        proj_c(1, 0, wd, 0)
                        pe.wait_ge(s["proj_evac"], ev + T + 1)
                        proj_c(0, 0, wv, 0)
                        pe.wait_ge(s["proj_evac"], ev + T + 2)
                        proj_c(1, 0, wd, D)
                    else:
                        pe.wait_ge(s["v_evac"], vv + 1)
                        pe.wait_ge(s["proj_evac"], ev + T + 1 + t)
                        proj_c(0, t, wk, 0)
                        pe.wait_ge(s["v_evac"], vv + t + 1)
                        proj_c(1, t, wv, 0)

                def transpose_blocks(u):
                    pe.wait_ge(s["blk_set"], b * NU + u + 1)
                    for half in range(2):
                        if u == 0:
                            pe.wait_ge(s["xT_lo"], b * NX2 + T)
                        elif half == 0:
                            pe.wait_ge(s["blk_act"], b * NU + u)
                        else:
                            pe.wait_ge(s["blk_dve"], b * NU + u)
                        for j in range(HALF):
                            last = pe.transpose(pTh[half][0:96, j, :], blk[u % 2][:, half * HALF + j, :], ident_h[:, :])
                        last.then_inc(s["blk_ps"], 1)

                for t in range(T):
                    transpose_x(t)
                for u in range(NU + 2):
                    if u < T:
                        proj_q(u)
                    elif u < NU:
                        proj_kv(u - T)
                    if u >= 2:
                        transpose_blocks(u - 2)

                pe.wait_ge(s["blk_act"], (b + 1) * NU)
                pe.wait_ge(s["blk_dve"], (b + 1) * NU)
                for m in range(NS):
                    t, p = divmod(m, H // 2)
                    if m >= 2:
                        pe.wait_ge(s["S_exp"], b * NS + m - 1)
                    for j in range(2):
                        h = 2 * p + j
                        last = pe.matmul(pS[m % 2][:, j, :], qT[0:96, h, t * P:(t + 1) * P], kT[0:96, h, :], start=True, stop=True)
                    last.then_inc(s["S_done"], 1)
                pe.wait_ge(s["c_set"], b + 1)
                for half in range(2):
                    for t in range(T):
                        last = pe.transpose(pT[0][96:P, :].bitcast(F16)[:, half * S + t * P:half * S + (t + 1) * P],
                                            caug[:, t, half * HALF:(half + 1) * HALF].rearrange("p h a c -> p (h a c)"), ident_h[:, :])
                last.then_inc(s["aug_ps"], 1)
                pe.wait_ge(s["aug_act"], b + 1)
                pe.wait_ge(s["aug_dve"], b + 1)

                def scores_t(n_):
                    g, kt = divmod(n_, T)
                    for p in range(2):
                        r = 2 * n_ + p
                        if r < 2:
                            pe.wait_ge(s["S_exp"], (b + 1) * NS)
                        else:
                            pe.wait_ge(s["probs_set"], b * (2 * G * T) + r - 1)
                        for j in range(2):
                            h = g * HG + 2 * p + j
                            last = pe.matmul(pS[r % 2][:, j, :], kT[:, h, kt * P:(kt + 1) * P], qT[:, h, :], start=True, stop=True)
                        last.then_inc(s["ST_done"], 1)

                def weigh_values(n_):
                    g, kt = divmod(n_, T)
                    pe.wait_ge(s["probs_set"], b * (2 * G * T) + 2 * n_ + 2)
                    if kt == 0:
                        if g < 2:
                            pe.wait_ge(s["proj_evac"], (b + 1) * (NU + 1))
                            pe.wait_ge(s["v_evac"], (b + 1) * (T + 1))
                        else:
                            pe.wait_ge(s["aT_lo"], b * G + g - 1)
                    for j in range(HG):
                        h = g * HG + j
                        last = pe.matmul(pJ[g % 2][j * HD:(j + 1) * HD, :], v_sb[:, kt, h * HD:(h + 1) * HD], probs[n_ % 2][:, j, :],
                                         start=(kt == 0), stop=(kt == T - 1), tile_position=(0, j * HD))
                    last.then_inc(s["pv_done"], 1)

                for n_ in range(G * T + 1):
                    if n_ < G * T:
                        scores_t(n_)
                    if n_:
                        weigh_values(n_ - 1)

                for t in range(T):
                    pe.wait_ge(s["aT_lo"], (b + 1) * G)
                    if t >= 2:
                        pe.wait_ge(s["x2_set"], b * T + t - 1)
                    product(pJ[t % 2][:, :], lambda a, i: aT[a][:, i, t * P:(t + 1) * P], lambda c, i: wo[c][:, i, :], G)\
                        .then_inc(s["wo_done"], 1)
                for t in range(T):
                    transpose_x(T + t)

                pe.wait_ge(s["xT_lo"], (b + 1) * NX2)
                for it in range(IT):
                    m = P if it < IT - 1 else LAST
                    if it < 2:
                        pe.wait_ge(s["probs_set"], (b + 1) * (2 * G * T))
                    else:
                        pe.wait_ge(s["h_set"], b * IT + it - 1)
                    wf = (wf_hi, wf_lo)
                    for o, c0 in ((0, 0), (1, UP0)):
                        last = product(pS[it % 2][0:m, o, :],
                                       lambda a, i: wf[a][:, c0 + i * INTER + it * P:c0 + i * INTER + it * P + m],
                                       lambda c, i: xT[c][:, i, :], KQ)
                    last.then_inc(s["gu_done"], 1)
                for t in range(T):
                    if t < 2:
                        pe.wait_ge(s["x2_set"], (b + 1) * T)
                    else:
                        pe.wait_ge(s["y_set"], b * T + t - 1)
                    rows = lambda i: P if i < IT - 1 else LAST
                    product(pJ[t % 2][:, :], lambda a, i: hT[a][0:rows(i), i, t * P:(t + 1) * P],
                            lambda c, i: wf[c][0:rows(i), DN0 + i * D:DN0 + (i + 1) * D], IT,
                            wait=(lambda i: pe.wait_ge(s["h_lo"], b * IT + i + 1)) if t == 0 else None).then_inc(s["down_done"], 1)


def kernel(**inputs):
    import numpy as np
    import concourse.bacc as bacc
    from concourse.bass_utils import run_bass_kernel_spmd

    nc = bacc.Bacc("TRN2", target_bir_lowering=False, num_devices=1)
    src = {k.replace("L0_xattn_", "").replace("L0_ffn_", ""): np.asarray(v) for k, v in inputs.items()}
    arrays, args = {}, {}

    def give(name, a):
        a = np.ascontiguousarray(a)
        arrays[f"in_{name}"] = a
        args[name] = nc.dram_tensor(f"in_{name}", a.shape, mybir.dt.from_np(a.dtype), kind="ExternalInput").ap()

    for name in ("x", "Wq", "bq", "Wkv_dca", "bkv_dca", "qn_w", "qn_b", "kn_w", "kn_b", "kn_dca_w", "kn_dca_b", "Wo", "bo", "lut"):
        give(name, src[name])
    w = np.concatenate([src["Wk"], src["Wv"]], axis=1).reshape(KD, H, 2, HD)
    give("Wk", w[:, :, 0].reshape(KD, D))
    give("Wv", w[:, :, 1].reshape(KD, D))
    bias = np.concatenate([src["bk"], src["bv"]]).reshape(H, 2, HD)
    give("bk", bias[:, 0].reshape(D))
    give("bv", bias[:, 1].reshape(G, P).T)
    give("bvd", src["bkv_dca"][D:].reshape(G, P).T)
    c = src["ctx_1024"]
    give("ctxT", np.concatenate([c[:, S - DCA:], c[:, :S - DCA]], axis=1).transpose(0, 2, 1))
    gate = src["gate_idx"].T.reshape(KQ, P, INTER).transpose(1, 0, 2).reshape(P, KQ * INTER)
    up = src["up_idx"].T.reshape(KQ, P, INTER).transpose(1, 0, 2).reshape(P, KQ * INTER)
    down = np.pad(src["down_idx"].T, ((0, IT * P - INTER), (0, 0))).reshape(IT, P, D).transpose(1, 0, 2).reshape(P, IT * D)
    give("idx", np.concatenate([gate, up, down], axis=1))
    out = nc.dram_tensor("out", (B, S, D), F32, kind="ExternalOutput").ap()
    xattn_ffn(nc, args, out)
    r = run_bass_kernel_spmd(nc, [arrays], core_ids=[0])
    return r.results[0]["out"]
```

```python
from contextlib import ExitStack

import concourse.bass as bass
from concourse import mybir

F32 = mybir.dt.float32
F16 = mybir.dt.float16
I32 = mybir.dt.int32
U16 = mybir.dt.uint16
ALU = mybir.AluOpType
ACT = mybir.ActivationFunctionType
AX_X = mybir.AxisListType.X

P = 128
B, S, D = 4, 512, 512
KD = 256
H, HD = 16, 32
DCA = 16
INTER = 1376
NLUT = 16
T = S // P
KQ, KC = D // P, KD // P
G = H * HD // P
HG = P // HD
HALF = H // 2
NU = 2 * T
NS = T * H // 2
NR = 2 * G * T
IT = -(-INTER // P)
LAST = INTER - (IT - 1) * P
WCOLS = 2 * KQ * INTER + IT * D
UP0, DN0 = KQ * INTER, 2 * KQ * INTER
NCH = 32
CH = WCOLS // NCH
QK_SCALE = float(HD) ** -0.5
WS = 256.0
EPS_X, EPS_H = 1e-5, 1e-6
RING = 5
DOWN = ((0, 4), (4, 8), (8, IT))
assert NCH * CH == WCOLS and T == 4

FFN = ([("gate_up", i) for i in range(0, 5)] + [("down", 0, 0), ("down", 0, 2)]
       + [("gate_up", i) for i in range(5, 9)] + [("down", 1, 0), ("down", 1, 2)]
       + [("gate_up", i) for i in range(9, IT)] + [("down", 2, 0), ("down", 2, 2)])
S_ONE = NU + 2
S_SHIFT = S_ONE + NS // 2
S_TWO = S_SHIFT + 2
FFN_SLOT = dict(zip((0, 1, 3, 5, 7, 9, 10, 12, 14, 16, 18, 20, 22, 24, 25, 26, 27), range(len(FFN))))
assert len(FFN_SLOT) == len(FFN) and S_TWO + G == NCH

TAIL_PE = "wo0 wo1 tr1_0 tr1_1 wo2 wo3 tr2_0 tr1_2 tr2_1 tr1_3 tr2_2 tr2_3".split()
TAIL_ACT = "hi1_0 hi1_1 ctx1 hi2_0 hi1_2 hi2_1 hi1_3 hi2_2 hi2_3".split()
TAIL_DVE = ("ln1_0 ln1_1 res0 res1 lo1_0 ln2_0 lo1_1 ln2_1 ctx1 ln1_2 res2 ln1_3 res3 lo2_0 lo1_2 lo2_1 lo1_3 "
            "ln2_2 ln2_3 lo2_2 lo2_3").split()
TAIL_POOL = "rs1_0 rs1_1 rs2_0 rs2_1 ctx1 rs1_2 rs1_3 rs2_2 rs2_3".split()


def steps(order, this, nxt):
    for name in order:
        first = name[2:].startswith("1_") or name == "ctx1"
        if (nxt if first else this) is not None:
            yield name[:2], (1 if first else 2), int(name[-1]), (nxt if first else this)


def nth(batch, per, k):
    base, ahead = batch
    return base * per + (ahead * per + k)


def xattn_ffn(nc, A, out):
    nc.disable_value_cache = True
    ctx = ExitStack()
    with ctx:
        def sb(name, shape, dt):
            return ctx.enter_context(nc.sbuf_tensor(name, shape, dt))

        wf_hi = sb("wf_hi", [P, WCOLS], F16)
        wf_lo = sb("wf_lo", [P, WCOLS], F16)
        wq = [sb(f"wq{i}", [P, KQ, D], F16) for i in range(2)]
        wk = [sb(f"wk{i}", [P, KC, D], F16) for i in range(2)]
        wv = [sb(f"wv{i}", [P, KC, D], F16) for i in range(2)]
        wd = [sb(f"wd{i}", [P, KC, 2 * D], F16) for i in range(2)]
        wo = [sb(f"wo{i}", [P, G, D], F16) for i in range(2)]
        b16 = {n: sb("b16_" + n, [P, D], F16) for n in ("q", "k", "d", "o")}
        ones = sb("ones", [P, P], F16)
        ones_m = sb("ones_m", [P, P], F16)
        ones_d = sb("ones_d", [P, P], F16)
        bvm, bvd, bvs = (sb(n, [P, G], F32) for n in ("bvm", "bvd", "bvs"))
        lnw = {n: sb("ln_" + n, [P, HD], F32) for n in ("qw", "qb", "kw", "kb", "kw0", "kb0")}
        ident = sb("ident", [P, P], F32)
        ident_h = sb("ident_h", [P, P], F16)
        lut = sb("lut", [P, NLUT], F32)
        lut_d = sb("lut_d", [P, NLUT // 2], F32)
        mhalf = sb("mhalf", [P, H], F32)
        cmean = sb("cmean", [P, 64], F32)
        idle = sb("idle", [P, 2], F32)
        stat = sb("stat", [P, 2, 2, 6], F32)
        mv = sb("mv", [P, 2, 2, 2], F32)
        xvar = sb("xvar", [P, 2, 2], F32)
        xrstd = sb("xrstd", [P, 2, 2], F32)
        hvar = sb("hvar", [P, 2, H], F32)
        hrstd = sb("hrstd", [P, 2, H], F32)
        nmax = sb("nmax", [P, 2, T, H], F32)
        den = sb("den", [P, 2, T, H], F32)
        shift = sb("shift", [P, 2, T, H], F32)
        caug = sb("caug", [P, T, H, 2, 2], F16)

        words = 50 * 512
        arena = sb("arena", [P, words], F32)
        at = [0]

        def cut(n):
            a = at[0]
            at[0] += n
            assert at[0] <= words, at[0]
            return arena[:, a:a + n]

        def tiles16(n):
            return [cut(n * S // 2).bitcast(F16).rearrange("p (k s) -> p k s", k=n) for _ in range(2)]

        xs = [cut(D) for _ in range(2)]
        blk = [cut(H * 96 // 2).bitcast(F16).rearrange("p (h c) -> p h c", h=H) for _ in range(2)]
        qn = [cut(D) for _ in range(2)]
        a_stage = at[0]
        qT = cut(H * S // 2).bitcast(F16).rearrange("p (h s) -> p h s", h=H)
        a_v = at[0]
        v_sb = cut(T * D).rearrange("p (t n) -> p t n", t=T)
        ctx_raw = arena[:, a_v:a_v + KC * S]
        a_p = at[0]
        probs = [cut(HG * S).rearrange("p (j s) -> p j s", j=HG) for _ in range(2)]
        a_end = at[0]
        sd = arena[:, a_p:a_p + T * H * DCA].rearrange("p (r k) -> p r k", k=DCA)
        at[0] = a_p
        cT = tiles16(KC)
        c0 = {n: [cut(KC * P // 2).bitcast(F16).rearrange("p (k s) -> p k s", k=KC) for _ in range(2)] for n in "md"}
        at[0] = a_end - 2 * KQ * S // 2
        xT = tiles16(KQ)
        assert at[0] == a_end
        kT = cut(H * S // 2).bitcast(F16).rearrange("p (h s) -> p h s", h=H)
        a_f = at[0]
        x2 = cut(T * D).rearrange("p (t n) -> p t n", t=T)
        xT2 = tiles16(KQ)
        hT = tiles16(RING)
        sg = [cut(D) for _ in range(2)]
        assert at[0] == words
        aT = [[qT[:, HG * g + i, :] for g in range(G)] for i in range(2)]

        at[0] = a_stage
        st_q = cut(KQ * D)
        st_kv = [cut(KC * D) for _ in range(2)]
        st_o = cut(G * D)
        at[0] = a_stage + 6144
        st_d = cut(KC * 2 * D)
        assert at[0] <= a_end - 2 * KQ * S // 2
        pat = [blk[i].rearrange("p h c -> p (h c)")[:, 0:HALF * HD].rearrange("p (h c) -> p h c", h=HALF) for i in range(2)]
        at[0] = a_f
        l_leaf = [cut(CH) for _ in range(8)]
        l_w = [l_leaf[0], cut(CH)]
        l_idx = [cut(CH).bitcast(I32) for _ in range(2)]
        l_b0 = [cut(CH).bitcast(I32) for _ in range(2)]
        l_m = [cut(CH // 2).bitcast(U16) for _ in range(3)]
        st_b = {n: l_leaf[i][:, 0:D] for i, n in enumerate("qkdo")}

        ps = ctx.enter_context(nc.psum_tensor("ps", [P, 8, 512], F32))
        SC, VB, TB, AB, FB = 0, 0, 2, 4, 6
        ps16 = lambda bank: ps[:, bank, :].bitcast(F16)

        names = """wq_in wkv_in wd_in wo_in small_in lut_in idx_in0 idx_in1
            ident_set pat_set pat_ps pat_copied pool_chain dve_chain w_hi w_cent w_lo bias_set lut_ready
            b0_set mask_set leaf_act leaf_pool tree_a tree_chain l_selected l_hi l_lo
            x_in0 x_in1 ctx_in res_in out_stored cT_hi cT_lo c0_zero c0_set
            stat1 mean1 var1 rstd1 xn1 ps1 hi1 lo1 stat2 mean2 var2 rstd2 xn2 ps2 hi2 lo2
            proj_done v_done v_evac sq_set hsum_set hvar_set hrstd_set qc_set mul_set qn_set blk_hi blk_set blk_ps blk_act blk_dve
            S_done max_set S_exp dca_max sd_set ed_set den_set ln_set shift_set c_hi c_set aug_ps aug_act aug_dve
            ST_done probs_set pv_done aT_hi aT_lo wo_done x2_set
            gate_done up_done tanh_set gate_used h_set h_hi h_lo down_done down_evac""".split()
        s = {n: ctx.enter_context(nc.semaphore(n)) for n in names}

        heads = lambda a: a.rearrange("p (h d) -> p h d", d=HD)
        rows = lambda it: P if it < IT - 1 else LAST

        block = ctx.enter_context(nc.Block())

        @block.sync
        def _(sp):
            def row(name, lo, hi):
                return A[name][lo:hi].rearrange("(o n) -> o n", o=1)

            def load_x(batch, t, src):
                sp.dma_start(xs[t % 2], src).then_inc(s[f"x_in{t % 2}"], 16)

            flat = A["x"].rearrange("b s n -> (b s n)")
            flat_out = out.rearrange("b s n -> (b s n)")
            tile_of = lambda a, first: a[bass.ds(first, P * D)].rearrange("(p n) -> p n", n=D)
            xaddr = lambda base, ahead, t: base * (S * D) + (ahead * (S * D) + t * (P * D))

            for t in range(2):
                load_x((0, 0), t, tile_of(flat, xaddr(0, 0, t)))
            sp.dma_start(st_q.rearrange("p (k n) -> p k n", k=KQ),
                         A["Wq"].rearrange("(k p) n -> p k n", p=P)).then_inc(s["wq_in"], 16)
            for i, n in enumerate(("Wk", "Wv")):
                sp.dma_start(st_kv[i].rearrange("p (k n) -> p k n", k=KC),
                             A[n].rearrange("(k p) n -> p k n", p=P)).then_inc(s["wkv_in"], 16)
            sp.dma_start(lut[:, :], row("lut", 0, NLUT).to_broadcast([P, NLUT])).then_inc(s["lut_in"], 16)
            for n, src in (("q", row("bq", 0, D)), ("k", row("bk", 0, D)), ("d", row("bkv_dca", 0, D)), ("o", row("bo", 0, D))):
                sp.dma_start(st_b[n], src.to_broadcast([P, D])).then_inc(s["small_in"], 16)
            sp.dma_start(bvm[:, :], A["bv"]).then_inc(s["small_in"], 16)
            sp.dma_start(bvd[:, :], A["bvd"]).then_inc(s["small_in"], 16)
            for key, name in (("qw", "qn_w"), ("qb", "qn_b"), ("kw", "kn_w"), ("kb", "kn_b")):
                sp.dma_start(lnw[key][:, :], row(name, 0, HD).to_broadcast([P, HD])).then_inc(s["small_in"], 16)
            for key, name in (("kw0", "kn_w"), ("kb0", "kn_b")):
                sp.dma_start(lnw[key][DCA:P, :], row(name, 0, HD).to_broadcast([P - DCA, HD])).then_inc(s["small_in"], 16)
            for key, name in (("kw0", "kn_dca_w"), ("kb0", "kn_dca_b")):
                sp.dma_start(lnw[key][0:DCA, :], row(name, 0, HD).to_broadcast([DCA, HD])).then_inc(s["small_in"], 16)
            sp.dma_start(st_d.rearrange("p (k n) -> p k n", k=KC),
                         A["Wkv_dca"].rearrange("(k p) n -> p k n", p=P)).then_inc(s["wd_in"], 16)
            sp.dma_start(st_o.rearrange("p (k n) -> p k n", k=G),
                         A["Wo"].rearrange("(k p) n -> p k n", p=P)).then_inc(s["wo_in"], 16)
            for c in range(2):
                sp.dma_start(l_idx[c], A["idx"][:, c * CH:(c + 1) * CH]).then_inc(s[f"idx_in{c}"], 16)
            for t in range(2, T):
                sp.wait_ge(s["ps1"], t - 1)
                load_x((0, 0), t, tile_of(flat, xaddr(0, 0, t)))
            sp.wait_ge(s["w_lo"], 5)
            sp.dma_start(ctx_raw.rearrange("p (k n) -> p k n", k=KC),
                         A["ctxT"][0].rearrange("(k p) n -> p k n", p=P)).then_inc(s["ctx_in"], 16)
            for c in range(2, NCH):
                sp.wait_ge(s["mask_set"], c - 1)
                sp.dma_start(l_idx[c % 2], A["idx"][:, c * CH:(c + 1) * CH]).then_inc(s[f"idx_in{c % 2}"], 16)

            def load_residual(b, first, last):
                if first:
                    sp.wait_ge(s["l_lo"], NCH)
                elif last:
                    sp.wait_ge(s["out_stored"], 16 * T * (B - 1))
                else:
                    sp.wait_ge(s["out_stored"], sp.snap(b * (16 * T)))
                sp.dma_start(x2, A["x"][bass.ds(b, 1)].rearrange("a (t p) n -> p (a t) n", p=P)).then_inc(s["res_in"], 16)

            def store(b, static):
                val = (lambda v: v) if static else sp.snap
                for t in range(T):
                    dst = tile_of(flat_out, val(xaddr(b, 0, t)))
                    sp.wait_ge(s["down_evac"], val(b * (3 * T) + (2 * T + t + 1)))
                    sp.dma_start(dst, x2[:, t, :]).then_inc(s["out_stored"], 16)

            def batch(b, first):
                val = (lambda v: v) if first else sp.snap
                load_residual(b, first, False)
                src = [tile_of(flat, val(xaddr(b, 1, t))) for t in range(T)]
                sp.wait_ge(s["hsum_set"], val(b * NU + NU))
                load_x((b, 1), 0, src[0])
                load_x((b, 1), 1, src[1])
                sp.wait_ge(s["pv_done"], val(b * (G * T) + G * T))
                sp.dma_start(ctx_raw.rearrange("p (k n) -> p k n", k=KC),
                             A["ctxT"][bass.ds(val(b + 1), 1)].rearrange("a (k p) n -> p (a k) n", p=P)).then_inc(s["ctx_in"], 16)
                for t in range(2, T):
                    sp.wait_ge(s["ps1"], val(b * T + (T + t - 1)))
                    load_x((b, 1), t, src[t])
                store(b, first)

            batch(0, True)
            with sp.Fori(1, B - 1) as b:
                batch(b, False)
            load_residual(B - 1, False, True)
            store(B - 1, True)
            sp.wait_ge(s["out_stored"], 16 * T * B)

        @block.gpsimd
        def _(pool):
            n = [0]

            def take_wait():
                pool.tensor_tensor(idle[:, 0:1], mhalf[:, 0:1], mhalf[:, 0:1], ALU.mult)

            def link(ins):
                n[0] += 1
                ins.then_inc(s["pool_chain"], 1)
                pool.wait_ge(s["pool_chain"], n[0])

            pool.memset(mhalf[:, :], -0.5).then_inc(s["ident_set"], 1)
            link(pool.memset(ident[:, :], 0.0))
            pool.affine_select(out=ident[:, :], in_=ident[:, :], compare_op=ALU.not_equal, fill=1.0, base=0,
                               pattern=[[-1, P]], channel_multiplier=1).then_inc(s["ident_set"], 1)
            link(pool.memset(ident_h[:, :], 0.0))
            pool.affine_select(out=ident_h[:, :], in_=ident_h[:, :], compare_op=ALU.not_equal, fill=1.0, base=0,
                               pattern=[[-1, P]], channel_multiplier=1).then_inc(s["ident_set"], 1)
            pool.memset(ones[:, :], 1.0 / 64)
            link(pool.memset(ones_m[:, :], 1.0 / 64))
            link(pool.memset(ones_d[:, :], 0.0))
            pool.memset(ones_m[:, 0:DCA], 0.0)
            pool.memset(ones_d[:, 0:DCA], 1.0 / 64).then_inc(s["ident_set"], 1)
            link(pool.memset(pat[0], 0.0))
            link(pool.memset(pat[1], 0.0))
            for j in range(HALF):
                for i in range(2):
                    link(pool.memset(pat[i][:, j, 4 * j:4 * j + 2], 1.0))
                link(pool.memset(pat[0][0:DCA, j, 4 * j:4 * j + 2], 0.0))
                link(pool.memset(pat[0][0:DCA, j, 4 * j + 2:4 * j + 4], 1.0))
            pool.memset(cmean[:, 0:1], 0.0).then_inc(s["pat_set"], 1)

            def lookup(c):
                pool.wait_ge(s["b0_set"], c + 1)
                if c:
                    pool.wait_ge(s["l_selected"], c)
                else:
                    pool.wait_ge(s["lut_ready"], 2)
                    pool.wait_ge(s["bias_set"], 4)
                for j in range(4, 8):
                    last = pool.tensor_scalar(l_leaf[j], l_b0[c % 2], lut_d[:, j:j + 1], lut[:, 2 * j:2 * j + 1],
                                              ALU.mult, ALU.add)
                last.then_inc(s["leaf_pool"], 1)
                if c:
                    lookup_low(c - 1)

            def lookup_low(c):
                cols = slice(c * CH, (c + 1) * CH)
                pool.wait_ge(s["l_hi"], c + 1)
                pool.tensor_tensor(wf_lo[:, cols], l_w[c % 2], wf_hi[:, cols], ALU.subtract).then_inc(s["l_lo"], 1)

            def ffn(f, piece):
                if piece[0] == "gate_up":
                    it = piece[1]
                    m = rows(it)
                    pool.wait_ge(s["h_set"], nth(f, IT, it + 1))
                    take_wait()
                    pool.tensor_scalar(hT[0][0:m, it % RING, :], sg[it % 2][0:m, :], 1.0, 0.0, ALU.mult, ALU.add)\
                        .then_inc(s["h_hi"], 1)

            def end(this, nxt):
                for what, kind, t, bt in steps(TAIL_POOL, this, nxt):
                    if what == "rs":
                        i = t % 2
                        pool.wait_ge(s[f"var{kind}"], nth(bt, T, t + 1))
                        pool.tensor_tensor(xrstd[:, kind - 1, i:i + 1], xvar[:, kind - 1, i:i + 1], mhalf[:, 0:1],
                                           ALU.pow).then_inc(s[f"rstd{kind}"], 1)
                    else:
                        pool.wait_ge(s["cT_lo"], nth(bt, 1, 1))
                        take_wait()
                        for i in range(2):
                            pool.memset(c0["m"][i], 0.0)
                            last = pool.memset(c0["d"][i], 0.0)
                        last.then_inc(s["c0_zero"], 1)
                        pool.wait_ge(s["c0_zero"], nth(bt, 1, 1))
                        take_wait()
                        for i in range(2):
                            pool.tensor_scalar(c0["m"][i][:, :, DCA:P], cT[i][:, :, DCA:P], 1.0, 0.0, ALU.mult, ALU.add)
                            last = pool.tensor_scalar(c0["d"][i][:, :, 0:DCA], cT[i][:, :, 0:DCA], 1.0, 0.0, ALU.mult, ALU.add)
                        last.then_inc(s["c0_set"], 1)

            def core(a, between):
                def rstd(u):
                    pool.wait_ge(s["hvar_set"], nth(a, NU, u + 1))
                    pool.tensor_tensor(hrstd[:, u % 2, :], hvar[:, u % 2, :], mhalf[:, :], ALU.pow).then_inc(s["hrstd_set"], 1)

                def scale(u):
                    w, bb = ((lnw["qw"], lnw["qb"]) if u < T else (lnw["kw0"], lnw["kb0"]) if u == T
                             else (lnw["kw"], lnw["kb"]))
                    v3 = heads(qn[u % 2])
                    pool.wait_ge(s["qc_set"], nth(a, NU, u + 1))
                    pool.tensor_tensor(v3, v3, w[:, :].unsqueeze(1).to_broadcast([P, H, HD]), ALU.mult).then_inc(s["mul_set"], 1)
                    pool.wait_ge(s["mul_set"], nth(a, NU, u + 1))
                    pool.tensor_tensor(v3, v3, bb[:, :].unsqueeze(1).to_broadcast([P, H, HD]), ALU.add).then_inc(s["qn_set"], 1)

                rstd(0)
                for u in range(NU + 2):
                    if u + 1 < NU:
                        rstd(u + 1)
                    if u < NU:
                        scale(u)
                    between(u)
                for slot in range(S_ONE, NCH):
                    between(slot)

            end(None, (0, 0))
            core((0, 0), lookup)
            lookup_low(NCH - 1)
            with pool.Fori(0, B - 1) as b:
                end((b, 0), (b, 1))
                core((b, 1), lambda slot: ffn((b, 0), FFN[FFN_SLOT[slot]]) if slot in FFN_SLOT else None)
            end((B - 1, 0), None)
            for piece in FFN:
                ffn((B - 1, 0), piece)

        @block.scalar
        def _(act):
            fl = lambda a: a[:, :, :].rearrange("p k n -> p (k n)")
            act.wait_ge(s["w_cent"], 1)
            act.activation(fl(wq[0]), st_q, ACT.Copy, scale=WS).then_inc(s["w_hi"], 1)
            act.wait_ge(s["w_cent"], 2)
            act.activation(fl(wk[0]), st_kv[0], ACT.Copy, scale=WS)
            act.activation(fl(wv[0]), st_kv[1], ACT.Copy, scale=WS).then_inc(s["w_hi"], 1)
            act.wait_ge(s["w_cent"], 3)
            act.activation(fl(wd[0]), st_d, ACT.Copy, scale=WS).then_inc(s["w_hi"], 1)
            act.wait_ge(s["wo_in"], 16)
            act.activation(fl(wo[0]), st_o, ACT.Copy, scale=WS).then_inc(s["w_hi"], 1)
            act.wait_ge(s["pat_ps"], 2)
            for t in range(T):
                for half in range(2):
                    act.activation(kT[96:P, half * HALF:(half + 1) * HALF, t * P:(t + 1) * P],
                                   ps16(FB + min(t, 1))[96:P, :].rearrange("p (h s) -> p h s", h=HALF), ACT.Copy)\
                       .then_inc(s["pat_copied"], 1)

            def lookup(c):
                act.wait_ge(s["b0_set"], c + 1)
                if c == 0:
                    act.wait_ge(s["lut_ready"], 2)
                    act.wait_ge(s["bias_set"], 4)
                else:
                    act.wait_ge(s["tree_a"], c)
                if c >= 2:
                    act.wait_ge(s["l_lo"], c - 1)
                for j in range(4):
                    last = act.activation(l_w[c % 2] if j == 0 else l_leaf[j], l_b0[c % 2], ACT.Identity,
                                          scale=lut_d[:, j:j + 1], bias=lut[:, 2 * j:2 * j + 1])
                last.then_inc(s["leaf_act"], 1)
                if c:
                    lookup_high(c - 1)

            def lookup_high(c):
                act.wait_ge(s["l_selected"], c + 1)
                act.activation(wf_hi[:, c * CH:(c + 1) * CH], l_w[c % 2], ACT.Copy).then_inc(s["l_hi"], 1)

            def ffn(f, piece):
                if piece[0] == "gate_up":
                    it = piece[1]
                    m = rows(it)
                    act.wait_ge(s["gate_done"], nth(f, IT, it + 1))
                    if it >= 2:
                        act.wait_ge(s["h_lo"], nth(f, IT, it - 1))
                    act.activation(sg[it % 2][0:m, :], ps[0:m, FB, :], ACT.Tanh, scale=0.5 / WS).then_inc(s["tanh_set"], 1)

            def end(this, nxt):
                for what, kind, t, bt in steps(TAIL_ACT, this, nxt):
                    if what == "hi":
                        act.wait_ge(s[f"ps{kind}"], nth(bt, T, t + 1))
                        bank = (VB if kind == 1 else TB) + t % 2
                        act.activation((xT if kind == 1 else xT2)[0][:, :, t * P:(t + 1) * P],
                                       ps[:, bank, :].rearrange("p (k s) -> p k s", k=KQ), ACT.Copy).then_inc(s[f"hi{kind}"], 1)
                    else:
                        act.wait_ge(s["ctx_in"], nth(bt, 16, 16))
                        act.activation(cT[0].rearrange("p k s -> p (k s)"), ctx_raw, ACT.Copy).then_inc(s["cT_hi"], 1)

            def core(a, between):
                def square(u):
                    act.wait_ge(s["proj_done"], nth(a, NU, u + 1))
                    if u >= 2:
                        act.wait_ge(s["hsum_set"], nth(a, NU, u - 1))
                    act.activation(xs[u % 2], ps[:, AB + u % 2, :], ACT.Square, scale=1.0 / WS).then_inc(s["sq_set"], 1)

                def values(t):
                    act.wait_ge(s["v_done"], nth(a, T, t + 1))
                    act.activation(v_sb[:, t, :], ps[:, VB + t % 2, :], ACT.Copy, scale=1.0 / WS).then_inc(s["v_evac"], 1)

                def block_hi(u):
                    act.wait_ge(s["qn_set"], nth(a, NU, u + 1))
                    if u >= 2:
                        act.wait_ge(s["blk_ps"], nth(a, 2 * NU, 2 * (u - 1)))
                    src = heads(qn[u % 2])
                    o = blk[u % 2]
                    act.activation(o[:, :, 0:HD], src, ACT.Copy)
                    second = HD if u < T else 2 * HD
                    act.activation(o[:, :, second:second + HD], src, ACT.Copy).then_inc(s["blk_hi"], 1)

                def block_out(u):
                    act.wait_ge(s["blk_ps"], nth(a, 2 * NU, 2 * u + 1))
                    dst = qT if u < T else kT
                    t = u % T
                    act.activation(dst[0:96, 0:HALF, t * P:(t + 1) * P],
                                   ps16(TB)[0:96, :].rearrange("p (h s) -> p h s", h=HALF), ACT.Copy).then_inc(s["blk_act"], 1)

                square(0)
                for u in range(NU + 2):
                    if u + 1 < NU:
                        square(u + 1)
                        if u + 1 >= T:
                            values(u + 1 - T)
                    if 1 <= u <= NU:
                        block_hi(u - 1)
                    if u >= 2:
                        block_out(u - 2)
                    between(u)

                for m in range(NS):
                    t, p = divmod(m, H // 2)
                    act.wait_ge(s["max_set"], nth(a, NS, m + 1))
                    for j in range(2):
                        h = 2 * p + j
                        sc = ps[:, SC + 2 * (m % 3) + j, DCA:S]
                        last = act.activation(sc, sc, ACT.Exp, bias=nmax[:, 0, t, h:h + 1], accum_out=den[:, 0, t, h:h + 1])
                    last.then_inc(s["S_exp"], 1)
                    if m % 2:
                        between(S_ONE + m // 2)
                act.wait_ge(s["sd_set"], nth(a, 1, 1))
                sdf = sd.rearrange("p r k -> p (r k)")
                act.activation(sdf, sdf, ACT.Exp).then_inc(s["ed_set"], 1)
                act.wait_ge(s["den_set"], nth(a, 1, 1))
                act.wait_ge(s["S_exp"], nth(a, NS, NS))
                dfl = den[:, :, :, :].rearrange("p a t h -> p (a t h)")
                act.activation(dfl, dfl, ACT.Ln).then_inc(s["ln_set"], 1)
                between(S_SHIFT)
                between(S_SHIFT + 1)
                act.wait_ge(s["aug_ps"], nth(a, 1, 1))
                for half in range(2):
                    last = act.activation(qT[96:P, half * HALF, :], ps16(AB)[96:P, half * S:(half + 1) * S], ACT.Copy)
                last.then_inc(s["aug_act"], 1)

                def attn_hi(g):
                    act.wait_ge(s["pv_done"], nth(a, G * T, T * (g + 1)))
                    act.activation(aT[0][g], ps[:, AB + g % 2, :], ACT.Identity, bias=bvs[:, g:g + 1]).then_inc(s["aT_hi"], 1)

                for n_ in range(G * T):
                    for p in range(2):
                        r = 2 * n_ + p
                        act.wait_ge(s["ST_done"], nth(a, NR, r + 1))
                        if p == 0 and n_ >= 2:
                            act.wait_ge(s["pv_done"], nth(a, G * T, n_ - 1))
                        bank = SC + 2 * (r % 2)
                        act.activation(probs[n_ % 2][:, 2 * p:2 * p + 2, :], ps[:, bank:bank + 2, :], ACT.Exp).then_inc(s["probs_set"], 1)
                    if n_ % T == 1 and n_ > T:
                        attn_hi(n_ // T - 1)
                    if n_ % T == T - 1:
                        between(S_TWO + n_ // T)
                attn_hi(G - 1)

            end(None, (0, 0))
            core((0, 0), lookup)
            lookup_high(NCH - 1)
            with act.Fori(0, B - 1) as b:
                end((b, 0), (b, 1))
                core((b, 1), lambda slot: ffn((b, 0), FFN[FFN_SLOT[slot]]) if slot in FFN_SLOT else None)
            end((B - 1, 0), None)
            for piece in FFN:
                ffn((B - 1, 0), piece)

        @block.vector
        def _(dve):
            n = [0]

            def take_wait():
                dve.memset(idle[:, 1:2], 0.0)

            def link(ins):
                n[0] += 1
                ins.then_inc(s["dve_chain"], 1)
                dve.wait_ge(s["dve_chain"], n[0])

            def centre(v):
                r = v.shape[1]
                link(dve.tensor_reduce(cmean[:, 0:r], v, AX_X, ALU.add))
                link(dve.tensor_scalar(cmean[:, 0:r], cmean[:, 0:r], 1.0 / HD, None, ALU.mult))
                return dve.tensor_tensor(v, v, cmean[:, 0:r].unsqueeze(2).to_broadcast([P, r, HD]), ALU.subtract)

            dve.wait_ge(s["pat_set"], 1)
            dve.wait_ge(s["wq_in"], 16)
            centre(heads(st_q)).then_inc(s["w_cent"], 1)
            dve.wait_ge(s["wkv_in"], 32)
            dve.wait_ge(s["w_cent"], 1)
            centre(heads(st_kv[0])).then_inc(s["w_cent"], 1)
            dve.wait_ge(s["wd_in"], 16)
            dk = st_d.rearrange("p (k n) -> p k n", k=KC)
            dve.wait_ge(s["w_cent"], 2)
            link(centre(heads(dk[:, 0, 0:D])))
            centre(heads(dk[:, 1, 0:D])).then_inc(s["w_cent"], 1)
            n_small = 4 + 2 + 4 + 2 + 2
            dve.wait_ge(s["small_in"], 16 * n_small)
            dve.wait_ge(s["w_cent"], 3)
            for b_ in "qkd":
                link(centre(heads(st_b[b_])))
            for b_ in "qkdo":
                link(dve.tensor_scalar(st_b[b_], st_b[b_], WS, None, ALU.mult))
                link(dve.tensor_scalar(b16[b_][:, :], st_b[b_], 1.0, None, ALU.mult))
                dve.tensor_tensor(b16[b_][64:P, :], st_b[b_][64:P, :], b16[b_][64:P, :], ALU.subtract).then_inc(s["bias_set"], 1)
            dve.tensor_scalar(lnw["qw"][:, :], lnw["qw"][:, :], QK_SCALE, None, ALU.mult)
            dve.tensor_scalar(lnw["qb"][:, :], lnw["qb"][:, :], QK_SCALE, None, ALU.mult)
            link(dve.tensor_tensor(bvs[:, :], bvm[:, :], bvd[:, :], ALU.add))
            dve.wait_ge(s["lut_in"], 16)
            link(dve.tensor_scalar(lut[:, :], lut[:, :], WS, None, ALU.mult))
            lp = lut[:, :].rearrange("p (j e) -> p j e", e=2)
            dve.tensor_tensor(lut_d[:, :], lp[:, :, 1], lp[:, :, 0], ALU.subtract).then_inc(s["lut_ready"], 2)
            fl = lambda a: a[:, :, :].rearrange("p k n -> p (k n)")

            def low(dst, src, hi):
                return dve.scalar_tensor_tensor(out=dst, in0=src, scalar=WS, in1=hi, op0=ALU.mult, op1=ALU.subtract)

            dve.wait_ge(s["w_hi"], 1)
            low(fl(wq[1]), st_q, fl(wq[0])).then_inc(s["w_lo"], 1)
            dve.wait_ge(s["w_hi"], 2)
            low(fl(wk[1]), st_kv[0], fl(wk[0])).then_inc(s["w_lo"], 1)
            low(fl(wv[1]), st_kv[1], fl(wv[0])).then_inc(s["w_lo"], 1)
            dve.wait_ge(s["w_hi"], 3)
            low(fl(wd[1]), st_d, fl(wd[0])).then_inc(s["w_lo"], 1)
            dve.wait_ge(s["w_hi"], 4)
            low(fl(wo[1]), st_o, fl(wo[0])).then_inc(s["w_lo"], 1)

            def lookup_bit0(c):
                dve.wait_ge(s[f"idx_in{c % 2}"], 16 * (c // 2 + 1))
                if c >= 2:
                    dve.wait_ge(s["leaf_act"], c - 1)
                    dve.wait_ge(s["leaf_pool"], c - 1)
                dve.tensor_scalar(l_b0[c % 2], l_idx[c % 2], 1, None, ALU.bitwise_and).then_inc(s["b0_set"], 1)

            TC = 4

            def lookup(c):
                if c + 1 < NCH:
                    lookup_bit0(c + 1)
                if c:
                    dve.wait_ge(s["l_selected"], c)
                low16 = l_idx[c % 2].bitcast(U16).rearrange("p (n e) -> p n e", e=2)[:, :, 0]
                for i in range(3):
                    last = dve.tensor_scalar(l_m[i], low16, 2 << i, None, ALU.bitwise_and)
                last.then_inc(s["mask_set"], 1)
                w = l_w[c % 2]
                L = l_leaf
                dve.wait_ge(s["mask_set"], c + 1)
                dve.wait_ge(s["leaf_act"], c + 1)
                dve.copy_predicated(w, l_m[0], L[1])
                dve.copy_predicated(L[2], l_m[0], L[3]).then_inc(s["tree_chain"], 1)
                dve.wait_ge(s["tree_chain"], c * TC + 1)
                dve.copy_predicated(w, l_m[1], L[2]).then_inc(s["tree_a"], 1)
                dve.wait_ge(s["leaf_pool"], c + 1)
                dve.copy_predicated(L[4], l_m[0], L[5])
                dve.copy_predicated(L[6], l_m[0], L[7]).then_inc(s["tree_chain"], 1)
                dve.wait_ge(s["tree_chain"], c * TC + 2)
                dve.copy_predicated(L[4], l_m[1], L[6]).then_inc(s["tree_chain"], 2)
                dve.wait_ge(s["tree_chain"], c * TC + TC)
                dve.copy_predicated(w, l_m[2], L[4]).then_inc(s["l_selected"], 1)

            def ffn_low(f, it):
                m = rows(it)
                dve.wait_ge(s["h_hi"], nth(f, IT, it + 1))
                dve.tensor_tensor(hT[1][0:m, it % RING, :], sg[it % 2][0:m, :], hT[0][0:m, it % RING, :], ALU.subtract)\
                   .then_inc(s["h_lo"], 1)

            def ffn(f, piece):
                if piece[0] == "gate_up":
                    it = piece[1]
                    m = rows(it)
                    g = sg[it % 2][0:m, :]
                    if it:
                        if it not in (5, 9):
                            ffn_low(f, it - 1)
                    dve.wait_ge(s["tanh_set"], nth(f, IT, it + 1))
                    dve.scalar_tensor_tensor(out=g, in0=g, scalar=1.0, in1=ps[0:m, FB, :], op0=ALU.add, op1=ALU.mult)\
                       .then_inc(s["gate_used"], 1)
                    dve.wait_ge(s["gate_used"], nth(f, IT, it + 1))
                    dve.wait_ge(s["up_done"], nth(f, IT, it + 1))
                    dve.scalar_tensor_tensor(out=g, in0=g, scalar=0.5 / (WS * WS), in1=ps[0:m, FB + 1, :], op0=ALU.mult,
                                             op1=ALU.mult).then_inc(s["h_set"], 1)
                else:
                    _, grp, t0 = piece
                    if t0 == 0:
                        ffn_low(f, (4, 8, IT - 1)[grp])
                    for t in (t0, t0 + 1):
                        dve.wait_ge(s["down_done"], nth(f, 3 * T, grp * T + t + 1))
                        if grp:
                            dve.wait_ge(s["down_evac"], nth(f, 3 * T, (grp - 1) * T + t + 1))
                        dve.scalar_tensor_tensor(out=x2[:, t, :], in0=ps[:, FB + t % 2, :], scalar=1.0 / WS, in1=x2[:, t, :],
                                                 op0=ALU.mult, op1=ALU.add).then_inc(s["down_evac"], 1)

            def end(this, nxt):
                for what, kind, t, bt in steps(TAIL_DVE, this, nxt):
                    i, kk = t % 2, kind - 1
                    if what == "ln":
                        src, dst = (xs[i], xs[i]) if kind == 1 else (x2[:, t, :], qn[i])
                        dve.wait_ge(s[f"x_in{i}"], nth(bt, 8 * T, 16 * (t // 2 + 1))) if kind == 1 else \
                            dve.wait_ge(s["x2_set"], nth(bt, T, t + 1))
                        if t >= 2:
                            dve.wait_ge(s[f"xn{kind}"], nth(bt, T, t - 1))
                        dve.bn_stats(stat[:, kk, i, :], src).then_inc(s[f"stat{kind}"], 1)
                        dve.wait_ge(s[f"stat{kind}"], nth(bt, T, t + 1))
                        take_wait()
                        dve.bn_aggr(mv[:, kk, i, :], stat[:, kk, i, :]).then_inc(s[f"mean{kind}"], 1)
                        dve.wait_ge(s[f"mean{kind}"], nth(bt, T, t + 1))
                        dve.tensor_scalar(xvar[:, kk, i:i + 1], mv[:, kk, i, 1:2], EPS_X, None, ALU.add).then_inc(s[f"var{kind}"], 1)
                        dve.wait_ge(s[f"rstd{kind}"], nth(bt, T, t + 1))
                        if t >= 2 and kind == 2:
                            dve.wait_ge(s["ps2"], nth(bt, T, t - 1))
                        dve.tensor_scalar(dst, src, mv[:, kk, i, 0:1], xrstd[:, kk, i:i + 1], ALU.subtract, ALU.mult)\
                           .then_inc(s[f"xn{kind}"], 1)
                    elif what == "lo":
                        dve.wait_ge(s[f"hi{kind}"], nth(bt, T, t + 1))
                        cols = slice(t * P, (t + 1) * P)
                        x_ = xT if kind == 1 else xT2
                        bank = (VB if kind == 1 else TB) + t % 2
                        dve.tensor_tensor(x_[1][:, :, cols], ps[:, bank, :].rearrange("p (k s) -> p k s", k=KQ),
                                          x_[0][:, :, cols], ALU.subtract).then_inc(s[f"lo{kind}"], 1)
                    elif what == "re":
                        dve.wait_ge(s["res_in"], nth(bt, 16, 16))
                        dve.wait_ge(s["wo_done"], nth(bt, T, t + 1))
                        dve.scalar_tensor_tensor(out=x2[:, t, :], in0=ps[:, AB + i, :], scalar=1.0 / WS, in1=x2[:, t, :],
                                                 op0=ALU.mult, op1=ALU.add).then_inc(s["x2_set"], 1)
                    else:
                        fc = lambda a_: a_.rearrange("p k s -> p (k s)")
                        dve.wait_ge(s["cT_hi"], nth(bt, 1, 1))
                        dve.tensor_tensor(fc(cT[1]), ctx_raw, fc(cT[0]), ALU.subtract).then_inc(s["cT_lo"], 1)

            def core(a, between):
                def variance(u):
                    i = u % 2
                    dve.wait_ge(s["sq_set"], nth(a, NU, u + 1))
                    if u >= 2:
                        dve.wait_ge(s["hrstd_set"], nth(a, NU, u - 1))
                    dve.tensor_reduce(hvar[:, i, :], heads(xs[i]), AX_X, ALU.add).then_inc(s["hsum_set"], 1)
                    dve.wait_ge(s["hsum_set"], nth(a, NU, u + 1))
                    dve.tensor_scalar(hvar[:, i, :], hvar[:, i, :], WS * WS / HD, EPS_H * WS * WS, ALU.mult, ALU.add)\
                       .then_inc(s["hvar_set"], 1)

                def normalise(u):
                    dve.wait_ge(s["hrstd_set"], nth(a, NU, u + 1))
                    if u >= 2:
                        dve.wait_ge(s["blk_set"], nth(a, NU, u - 1))
                    dve.tensor_tensor(heads(qn[u % 2]), heads(ps[:, AB + u % 2, :]),
                                      hrstd[:, u % 2, :].unsqueeze(2).to_broadcast([P, H, HD]), ALU.mult).then_inc(s["qc_set"], 1)

                def block_lo(u):
                    dve.wait_ge(s["blk_hi"], nth(a, NU, u + 1))
                    o = blk[u % 2]
                    c_0 = 2 * HD if u < T else HD
                    dve.tensor_tensor(o[:, :, c_0:c_0 + HD], heads(qn[u % 2]), o[:, :, 0:HD], ALU.subtract).then_inc(s["blk_set"], 1)

                def block_out(u):
                    dve.wait_ge(s["blk_ps"], nth(a, 2 * NU, 2 * u + 2))
                    dst = qT if u < T else kT
                    t = u % T
                    dve.tensor_copy(dst[0:96, HALF:H, t * P:(t + 1) * P],
                                    ps16(TB + 1)[0:96, :].rearrange("p (h s) -> p h s", h=HALF)).then_inc(s["blk_dve"], 1)

                variance(0)
                for u in range(NU + 2):
                    if u + 1 < NU:
                        variance(u + 1)
                    if 1 <= u <= NU:
                        block_lo(u - 1)
                    if u < NU:
                        normalise(u)
                    if u >= 2:
                        block_out(u - 2)
                    between(u)

                for m in range(NS):
                    t, p = divmod(m, H // 2)
                    dve.wait_ge(s["S_done"], nth(a, NS, m + 1))
                    sc = ps[:, SC + 2 * (m % 3):SC + 2 * (m % 3) + 2, :]
                    dve.tensor_reduce(nmax[:, 0, t, 2 * p:2 * p + 2], sc[:, :, DCA:S], AX_X, ALU.max, negate=True)
                    dve.tensor_copy(sd[:, t * H + 2 * p:t * H + 2 * p + 2, :], sc[:, :, 0:DCA]).then_inc(s["max_set"], 1)
                    if m % 2:
                        between(S_ONE + m // 2)
                dve.wait_ge(s["max_set"], nth(a, NS, NS))
                nm1 = nmax[:, 1, :, :].rearrange("p t h -> p (t h)")
                dve.tensor_reduce(nm1, sd, AX_X, ALU.max, negate=True).then_inc(s["dca_max"], 1)
                dve.wait_ge(s["dca_max"], nth(a, 1, 1))
                dve.tensor_tensor(sd, sd, nm1.unsqueeze(2).to_broadcast([P, T * H, DCA]), ALU.add).then_inc(s["sd_set"], 1)
                dve.wait_ge(s["ed_set"], nth(a, 1, 1))
                dve.tensor_reduce(den[:, 1, :, :].rearrange("p t h -> p (t h)"), sd, AX_X, ALU.add).then_inc(s["den_set"], 1)
                dve.wait_ge(s["ln_set"], nth(a, 1, 1))
                fs = lambda a_: a_[:, :, :, :].rearrange("p a t h -> p (a t h)")
                dve.tensor_tensor(fs(shift), fs(nmax), fs(den), ALU.subtract).then_inc(s["shift_set"], 1)
                dve.wait_ge(s["shift_set"], nth(a, 1, 1))
                for w in range(2):
                    last = dve.tensor_copy(caug[:, :, :, w, 0], shift[:, w, :, :])
                last.then_inc(s["c_hi"], 1)
                dve.wait_ge(s["c_hi"], nth(a, 1, 1))
                for w in range(2):
                    last = dve.tensor_tensor(caug[:, :, :, w, 1], shift[:, w, :, :], caug[:, :, :, w, 0], ALU.subtract)
                last.then_inc(s["c_set"], 1)
                between(S_SHIFT)
                between(S_SHIFT + 1)
                dve.wait_ge(s["aug_act"], nth(a, 1, 1))
                for half in range(2):
                    h0 = half * HALF
                    last = dve.tensor_copy(qT[96:P, h0 + 1:h0 + HALF, :],
                                           qT[96:P, h0:h0 + 1, :].to_broadcast([32, HALF - 1, S]))
                last.then_inc(s["aug_dve"], 1)

                for g in range(G):
                    between(S_TWO + g)
                    dve.wait_ge(s["aT_hi"], nth(a, G, g + 1))
                    dve.scalar_tensor_tensor(out=aT[1][g], in0=ps[:, AB + g % 2, :], scalar=bvs[:, g:g + 1], in1=aT[0][g],
                                             op0=ALU.add, op1=ALU.subtract).then_inc(s["aT_lo"], 1)

            end(None, (0, 0))
            lookup_bit0(0)
            core((0, 0), lookup)
            with dve.Fori(0, B - 1) as b:
                end((b, 0), (b, 1))
                core((b, 1), lambda slot: ffn((b, 0), FFN[FFN_SLOT[slot]]) if slot in FFN_SLOT else None)
            end((B - 1, 0), None)
            for piece in FFN:
                ffn((B - 1, 0), piece)

        @block.tensor
        def _(pe):
            pe.wait_ge(s["pat_set"], 1)
            pe.wait_ge(s["ident_set"], 4)
            for i in range(2):
                for j in range(HALF):
                    last = pe.transpose(ps16(FB + i)[96:P, j * P:(j + 1) * P], pat[i][:, j, :], ident_h[:, :])
                last.then_inc(s["pat_ps"], 1)

            def product(dst, terms, wait=None):
                todo = []
                for lhs, rhs in terms:
                    if isinstance(lhs, list):
                        todo += [(lhs[0], rhs[0]), (lhs[0], rhs[1]), (lhs[1], rhs[0])]
                    else:
                        todo.append((lhs, rhs))
                for i, (l, r) in enumerate(todo):
                    last = pe.matmul(dst, l, r, start=(i == 0), stop=(i == len(todo) - 1))
                return last

            both = lambda f: [f(0), f(1)]

            def ffn(f, piece):
                wf = (wf_hi, wf_lo)
                if piece[0] == "gate_up":
                    it = piece[1]
                    m = rows(it)
                    if it == 0:
                        pe.wait_ge(s["lo2"], nth(f, T, T))
                    if it in (5, 9):
                        pe.wait_ge(s["down_evac"], nth(f, 3 * T, T * (1 if it == 5 else 2)))
                    for o, c_0, used, done in ((0, 0, "gate_used", "gate_done"), (1, UP0, "h_set", "up_done")):
                        if it:
                            pe.wait_ge(s[used], nth(f, IT, it))
                        product(ps[0:m, FB + o, :],
                                [(both(lambda a_: wf[a_][:, c_0 + i * INTER + it * P:c_0 + i * INTER + it * P + m]),
                                  both(lambda a_: xT2[a_][:, i, :])) for i in range(KQ)]).then_inc(s[done], 1)
                else:
                    _, grp, t0 = piece
                    lo, hi = DOWN[grp]
                    if t0 == 0:
                        pe.wait_ge(s["h_lo"], nth(f, IT, hi))
                        pe.wait_ge(s["h_set"], nth(f, IT, (5, 9, IT)[grp]))
                    for t in (t0, t0 + 1):
                        if t >= 2:
                            pe.wait_ge(s["down_evac"], nth(f, 3 * T, grp * T + t - 1))
                        product(ps[:, FB + t % 2, :],
                                [(both(lambda a_: hT[a_][0:rows(i), i % RING, t * P:(t + 1) * P]),
                                  both(lambda a_: wf[a_][0:rows(i), DN0 + i * D:DN0 + (i + 1) * D])) for i in range(lo, hi)])\
                            .then_inc(s["down_done"], 1)

            def end(this, nxt):
                for what, kind, t, bt in steps(TAIL_PE, this, nxt):
                    if what == "wo":
                        if t == 0:
                            pe.wait_ge(s["aT_lo"], nth(bt, G, G))
                        if t >= 2:
                            pe.wait_ge(s["x2_set"], nth(bt, T, t - 1))
                        product(ps[:, AB + t % 2, :],
                                [(both(lambda a_: aT[a_][g][:, t * P:(t + 1) * P]), both(lambda a_: wo[a_][:, g, :])) for g in range(G)]
                                + [(ones[:, :], b16["o"][:, :])]).then_inc(s["wo_done"], 1)
                    else:
                        src = xs if kind == 1 else qn
                        bank = (VB if kind == 1 else TB) + t % 2
                        pe.wait_ge(s[f"xn{kind}"], nth(bt, T, t + 1))
                        if t >= 2:
                            pe.wait_ge(s[f"lo{kind}"], nth(bt, T, t - 1))
                        for k in range(KQ):
                            last = pe.transpose(ps[:, bank, k * P:(k + 1) * P], src[t % 2][:, k * P:(k + 1) * P], ident[:, :])
                        last.then_inc(s[f"ps{kind}"], 1)

            def core(a, between):
                def project(u):
                    t = u % T
                    cols = slice(t * P, (t + 1) * P)
                    if u >= 2:
                        pe.wait_ge(s["qc_set"], nth(a, NU, u - 1))
                    if u < T:
                        pe.wait_ge(s["lo1"], nth(a, T, t + 1))
                        product(ps[:, AB + u % 2, :],
                                [(both(lambda a_: xT[a_][:, i, cols]), both(lambda a_: wq[a_][:, i, :])) for i in range(KQ)]
                                + [(ones[:, :], b16["q"][:, :])]).then_inc(s["proj_done"], 1)
                        return
                    if t == 0:
                        pe.wait_ge(s["c0_set"], nth(a, 1, 1))
                        main, dca = c0["m"], c0["d"]
                        keys = [(both(lambda a_: main[a_][:, i, :]), both(lambda a_: wk[a_][:, i, :])) for i in range(KC)]
                        keys += [(both(lambda a_: dca[a_][:, i, :]), both(lambda a_: wd[a_][:, i, 0:D])) for i in range(KC)]
                        keys += [(ones_m[:, :], b16["k"][:, :]), (ones_d[:, :], b16["d"][:, :])]
                        vals = [(both(lambda a_: main[a_][:, i, :]), both(lambda a_: wv[a_][:, i, :])) for i in range(KC)]
                        vals += [(both(lambda a_: dca[a_][:, i, :]), both(lambda a_: wd[a_][:, i, D:2 * D])) for i in range(KC)]
                    else:
                        keys = [(both(lambda a_: cT[a_][:, i, cols]), both(lambda a_: wk[a_][:, i, :])) for i in range(KC)]
                        keys += [(ones[:, :], b16["k"][:, :])]
                        vals = [(both(lambda a_: cT[a_][:, i, cols]), both(lambda a_: wv[a_][:, i, :])) for i in range(KC)]
                    product(ps[:, AB + u % 2, :], keys).then_inc(s["proj_done"], 1)
                    if t == 0:
                        pe.wait_ge(s["lo1"], nth(a, T, T))
                    if t >= 2:
                        pe.wait_ge(s["v_evac"], nth(a, T, t - 1))
                    product(ps[:, VB + t % 2, :], vals).then_inc(s["v_done"], 1)

                def transpose_blocks(u):
                    pe.wait_ge(s["blk_set"], nth(a, NU, u + 1))
                    for half in range(2):
                        if u:
                            pe.wait_ge(s["blk_act" if half == 0 else "blk_dve"], nth(a, NU, u))
                        for j in range(HALF):
                            last = pe.transpose(ps16(TB + half)[0:96, j * P:(j + 1) * P], blk[u % 2][:, half * HALF + j, :], ident_h[:, :])
                        last.then_inc(s["blk_ps"], 1)

                project(0)
                for u in range(NU + 2):
                    if u + 1 < NU:
                        project(u + 1)
                    if u >= 2:
                        transpose_blocks(u - 2)
                    between(u)

                pe.wait_ge(s["blk_act"], nth(a, NU, NU))
                pe.wait_ge(s["blk_dve"], nth(a, NU, NU))
                pe.wait_ge(s["v_evac"], nth(a, T, T))
                for m in range(NS):
                    t, p = divmod(m, H // 2)
                    if m >= 3:
                        pe.wait_ge(s["S_exp"], nth(a, NS, m - 2))
                    for j in range(2):
                        h = 2 * p + j
                        last = pe.matmul(ps[:, SC + 2 * (m % 3) + j, :], qT[0:96, h, t * P:(t + 1) * P], kT[0:96, h, :], start=True, stop=True)
                    last.then_inc(s["S_done"], 1)
                    if m % 2:
                        between(S_ONE + m // 2)
                between(S_SHIFT)
                between(S_SHIFT + 1)
                pe.wait_ge(s["c_set"], nth(a, 1, 1))
                for half in range(2):
                    for t in range(T):
                        last = pe.transpose(ps16(AB)[96:P, half * S + t * P:half * S + (t + 1) * P],
                                            caug[:, t, half * HALF:(half + 1) * HALF].rearrange("p h a c -> p (h a c)"), ident_h[:, :])
                last.then_inc(s["aug_ps"], 1)
                pe.wait_ge(s["aug_dve"], nth(a, 1, 1))

                def scores_t(n_):
                    g, kt = divmod(n_, T)
                    for p in range(2):
                        r = 2 * n_ + p
                        if r >= 2:
                            pe.wait_ge(s["probs_set"], nth(a, NR, r - 1))
                        for j in range(2):
                            h = g * HG + 2 * p + j
                            last = pe.matmul(ps[:, SC + 2 * (r % 2) + j, :], kT[:, h, kt * P:(kt + 1) * P], qT[:, h, :], start=True, stop=True)
                        last.then_inc(s["ST_done"], 1)

                def weigh_values(n_):
                    g, kt = divmod(n_, T)
                    pe.wait_ge(s["probs_set"], nth(a, NR, 2 * n_ + 2))
                    if kt == 0 and g >= 2:
                        pe.wait_ge(s["aT_lo"], nth(a, G, g - 1))
                    for j in range(HG):
                        h = g * HG + j
                        last = pe.matmul(ps[j * HD:(j + 1) * HD, AB + g % 2, :], v_sb[:, kt, h * HD:(h + 1) * HD], probs[n_ % 2][:, j, :],
                                         start=(kt == 0), stop=(kt == T - 1), tile_position=(0, j * HD))
                    last.then_inc(s["pv_done"], 1)

                for n_ in range(G * T + 1):
                    if n_ < G * T:
                        scores_t(n_)
                    if n_:
                        weigh_values(n_ - 1)
                    if n_ % T == T - 1:
                        between(S_TWO + n_ // T)

            end(None, (0, 0))
            pe.wait_ge(s["w_lo"], 5)
            pe.wait_ge(s["bias_set"], 4)
            pe.wait_ge(s["pat_copied"], 2 * T)
            core((0, 0), lambda slot: None)
            pe.wait_ge(s["l_lo"], NCH)
            with pe.Fori(0, B - 1) as b:
                end((b, 0), (b, 1))
                core((b, 1), lambda slot: ffn((b, 0), FFN[FFN_SLOT[slot]]) if slot in FFN_SLOT else None)
            end((B - 1, 0), None)
            for piece in FFN:
                ffn((B - 1, 0), piece)


def kernel(**inputs):
    import numpy as np
    import concourse.bacc as bacc
    from concourse.bass_utils import run_bass_kernel_spmd

    nc = bacc.Bacc("TRN2", target_bir_lowering=False, num_devices=1)
    src = {k.replace("L0_xattn_", "").replace("L0_ffn_", ""): np.asarray(v) for k, v in inputs.items()}
    arrays, args = {}, {}

    def give(name, a):
        a = np.ascontiguousarray(a)
        arrays[f"in_{name}"] = a
        args[name] = nc.dram_tensor(f"in_{name}", a.shape, mybir.dt.from_np(a.dtype), kind="ExternalInput").ap()

    for name in ("x", "Wq", "bq", "Wkv_dca", "bkv_dca", "qn_w", "qn_b", "kn_w", "kn_b", "kn_dca_w", "kn_dca_b", "Wo", "bo", "lut"):
        give(name, src[name])
    w = np.concatenate([src["Wk"], src["Wv"]], axis=1).reshape(KD, H, 2, HD)
    give("Wk", w[:, :, 0].reshape(KD, D))
    give("Wv", w[:, :, 1].reshape(KD, D))
    bias = np.concatenate([src["bk"], src["bv"]]).reshape(H, 2, HD)
    give("bk", bias[:, 0].reshape(D))
    give("bv", bias[:, 1].reshape(G, P).T)
    give("bvd", src["bkv_dca"][D:].reshape(G, P).T)
    c = src["ctx_1024"]
    give("ctxT", np.concatenate([c[:, S - DCA:], c[:, :S - DCA]], axis=1).transpose(0, 2, 1))
    gate = src["gate_idx"].T.reshape(KQ, P, INTER).transpose(1, 0, 2).reshape(P, KQ * INTER)
    up = src["up_idx"].T.reshape(KQ, P, INTER).transpose(1, 0, 2).reshape(P, KQ * INTER)
    down = np.pad(src["down_idx"].T, ((0, IT * P - INTER), (0, 0))).reshape(IT, P, D).transpose(1, 0, 2).reshape(P, IT * D)
    give("idx", np.concatenate([gate, up, down], axis=1))
    out = nc.dram_tensor("out", (B, S, D), F32, kind="ExternalOutput").ap()
    xattn_ffn(nc, args, out)
    r = run_bass_kernel_spmd(nc, [arrays], core_ids=[0])
    return r.results[0]["out"]
```

```python
from contextlib import ExitStack

import concourse.bass as bass
from concourse import mybir

F32 = mybir.dt.float32
F16 = mybir.dt.float16
I32 = mybir.dt.int32
U16 = mybir.dt.uint16
ALU = mybir.AluOpType
ACT = mybir.ActivationFunctionType
AX_X = mybir.AxisListType.X

P = 128
B, S, D = 4, 512, 512
KD = 256
H, HD = 16, 32
DCA = 16
INTER = 1376
NLUT = 16
T = S // P
KQ, KC = D // P, KD // P
G = H * HD // P
HG = P // HD
HALF = H // 2
NU = 2 * T
NS = T * H // 2
NR = 2 * G * T
IT = -(-INTER // P)
LAST = INTER - (IT - 1) * P
WCOLS = 2 * KQ * INTER + IT * D
UP0, DN0 = KQ * INTER, 2 * KQ * INTER
NCH = 40
CH = WCOLS // NCH
QK_SCALE = float(HD) ** -0.5
WS = 256.0
EPS_X, EPS_H = 1e-5, 1e-6
RING = 5
DOWN = ((0, 4), (4, 8), (8, IT))
assert NCH * CH == WCOLS and T == 4

S_ONE = NU + 2
S_SHIFT = S_ONE + NS
S_TWO = S_SHIFT + 2
PRODUCTS = ([("gate_up", i) for i in range(0, 5)] + [("down", 0, 0), ("down", 0, 2)]
            + [("gate_up", i) for i in range(5, 9)] + [("down", 1, 0), ("down", 1, 2)]
            + [("gate_up", i) for i in range(9, IT)] + [("down", 2, 0), ("down", 2, 2)])
FFN_SLOT = dict(zip([1, 3, 5, 7, 9] + [S_ONE + m for m in (2, 5, 8, 11, 14, 17, 20, 22, 25, 27)] + [S_SHIFT, S_SHIFT + 1], PRODUCTS))
FFN_SLOT.update({slot + 1: ("low", p[1]) for slot, p in list(FFN_SLOT.items()) if p[0] == "gate_up"})
FFN = [FFN_SLOT[slot] for slot in sorted(FFN_SLOT)]
LOOKUP_SLOT = {slot: c for c, slot in enumerate(
    list(range(S_ONE)) + [S_ONE + i * NS // 20 for i in range(20)] + [S_SHIFT, S_SHIFT + 1] + [S_TWO + 2 * i for i in range(8)])}
assert len(FFN) == len(PRODUCTS) + IT and len(LOOKUP_SLOT) == NCH
AUG = ((0, 1, HG), (0, HG, HALF), (HALF, HALF + 1, H))
NORM_AT = {2: 0, 3: 1, 8: 2, 9: 3}
TURN_AT = {4: 0, 5: 1, 10: 2, 11: 3}


def nth(batch, per, k):
    base, ahead = batch
    return base * per + (ahead * per + k)


def xattn_ffn(nc, A, out):
    nc.disable_value_cache = True
    ctx = ExitStack()
    with ctx:
        def sb(name, shape, dt):
            return ctx.enter_context(nc.sbuf_tensor(name, shape, dt))

        wf_hi = sb("wf_hi", [P, WCOLS], F16)
        wf_lo = sb("wf_lo", [P, WCOLS], F16)
        wq = [sb(f"wq{i}", [P, KQ, D], F16) for i in range(2)]
        wk = [sb(f"wk{i}", [P, KC, D], F16) for i in range(2)]
        wv = [sb(f"wv{i}", [P, KC, D], F16) for i in range(2)]
        wd = [sb(f"wd{i}", [P, KC, 2 * D], F16) for i in range(2)]
        wo = [sb(f"wo{i}", [P, G, D], F16) for i in range(2)]
        b16 = {n: sb("b16_" + n, [P, D], F16) for n in ("q", "k", "d", "o")}
        ones = sb("ones", [P, P], F16)
        ones_m = sb("ones_m", [P, P], F16)
        ones_d = sb("ones_d", [P, P], F16)
        bvm, bvd, bvs = (sb(n, [P, G], F32) for n in ("bvm", "bvd", "bvs"))
        lnw = {n: sb("ln_" + n, [P, HD], F32) for n in ("qw", "qb", "kw", "kb", "kw0", "kb0")}
        ident = sb("ident", [P, P], F32)
        ident_h = sb("ident_h", [P, P], F16)
        lut = sb("lut", [P, NLUT], F32)
        lut_d = sb("lut_d", [P, NLUT // 2], F32)
        mhalf = sb("mhalf", [P, H], F32)
        cmean = sb("cmean", [P, 64], F32)
        idle = sb("idle", [P, 5], F32)
        stat = sb("stat", [P, 2, 2, 6], F32)
        mv = sb("mv", [P, 2, 2, 2], F32)
        xvar = sb("xvar", [P, 2, 2], F32)
        xrstd = sb("xrstd", [P, 2, 2], F32)
        hvar = sb("hvar", [P, 2, H], F32)
        hrstd = sb("hrstd", [P, 2, H], F32)
        nmax = sb("nmax", [P, 2, T, H], F32)
        den = sb("den", [P, 2, T, H], F32)
        shift = sb("shift", [P, 2, T, H], F32)
        caug = sb("caug", [P, T, H, 2, 2], F16)

        l_spare = sb("l_spare", [P, CH], F32)

        words = 50 * 512
        arena = sb("arena", [P, words], F32)
        at = [0]

        def cut(n):
            a = at[0]
            at[0] += n
            assert at[0] <= words, at[0]
            return arena[:, a:a + n]

        def tiles16(n):
            return [cut(n * S // 2).bitcast(F16).rearrange("p (k s) -> p k s", k=n) for _ in range(2)]

        xs = [cut(D) for _ in range(2)]
        blk = [cut(H * 96 // 2).bitcast(F16).rearrange("p (h c) -> p h c", h=H) for _ in range(2)]
        qn = [cut(D) for _ in range(2)]
        a_stage = at[0]
        qT = cut(H * S // 2).bitcast(F16).rearrange("p (h s) -> p h s", h=H)
        a_v = at[0]
        v_sb = cut(T * D).rearrange("p (t n) -> p t n", t=T)
        ctx_raw = arena[:, a_v:a_v + KC * S]
        a_p = at[0]
        probs = [cut(HG * S).rearrange("p (j s) -> p j s", j=HG) for _ in range(2)]
        a_end = at[0]
        sd = arena[:, a_p:a_p + T * H * DCA].rearrange("p (r k) -> p r k", k=DCA)
        at[0] = a_p
        cT = tiles16(KC)
        c0 = {n: [cut(KC * P // 2).bitcast(F16).rearrange("p (k s) -> p k s", k=KC) for _ in range(2)] for n in "md"}
        at[0] = a_end - KQ * S
        xT2 = tiles16(KQ)
        assert at[0] == a_end
        kT = cut(H * S // 2).bitcast(F16).rearrange("p (h s) -> p h s", h=H)
        xT = tiles16(KQ)
        a_x = at[0]
        x2 = cut(T * D).rearrange("p (t n) -> p t n", t=T)
        a_h = at[0]
        hT = tiles16(RING)
        ln2 = [arena[:, a_h + i * D:a_h + (i + 1) * D] for i in range(T)]
        sg = [cut(D) for _ in range(2)]
        assert at[0] == words
        aT = [[qT[:, HG * g + i, :] for g in range(G)] for i in range(2)]

        at[0] = a_stage
        st_q = cut(KQ * D)
        st_kv = [cut(KC * D) for _ in range(2)]
        st_o = cut(G * D)
        at[0] = a_stage + 6144
        st_d = cut(KC * 2 * D)
        assert at[0] <= a_end - KQ * S
        pat = [blk[i].rearrange("p h c -> p (h c)")[:, 0:HALF * HD].rearrange("p (h c) -> p h c", h=HALF) for i in range(2)]
        at[0] = a_x
        st_b = {n: cut(D) for n in "qkdo"}
        at[0] = a_x
        l_leaf = [cut(CH) for _ in range(8)]
        l_w = [l_leaf[0], cut(CH), l_spare[:, :]]
        l_idx = [cut(CH).bitcast(I32) for _ in range(2)]
        l_b0 = [cut(CH // 2).bitcast(U16) for _ in range(2)]
        l_m = [cut(CH // 2).bitcast(U16) for _ in range(3)]

        ps = ctx.enter_context(nc.psum_tensor("ps", [P, 8, 512], F32))
        SC, VB, TB, AB, FB = 0, 0, 2, 4, 6
        LB = ((FB, FB + 1, FB, FB + 1), (TB, TB + 1, FB, FB + 1))
        ps16 = lambda bank: ps[:, bank, :].bitcast(F16)

        names = """wq_in wkv_in wd_in wo_in small_in lut_in idx_in0 idx_in1
            ident_set pat_set pat_ps pat_copied pool_chain dve_chain w_hi w_cent b_cent w_lo bias_set lut_ready
            b0_set mask_set leaf_act leaf_pool pair_a pair_b tree_a tree_b l_selected l_hi l_lo
            x_in0 x_in1 ctx_in res_in out_stored cT_hi cT_lo c0_zero c0_set
            stat1 mean1 var1 rstd1 xn1 ps1 hi1 lo1 stat2 mean2 var2 rstd2 xn2 ps2 hi2 lo2
            proj_done v_done v_evac sq_set hsum_set hvar_set hrstd_set qc_set mul_set qn_set blk_hi blk_set blk_ps blk_act blk_dve
            S_done max_set S_exp dca_max sd_set ed_set den_set ln_set shift_set c_hi c_set aug_ps aug_act aug_dve
            ST_done probs_set pv_done aT_hi aT_lo wo_done x2_set
            gate_done up_done tanh_set gate_used h_set h_hi h_lo down_done down_evac""".split()
        s = {n: ctx.enter_context(nc.semaphore(n)) for n in names}

        heads = lambda a: a.rearrange("p (h d) -> p h d", d=HD)
        rows = lambda it: P if it < IT - 1 else LAST
        down_bank = lambda grp, t: TB + t % 2 if grp == 2 and t >= 2 else FB + t % 2

        block = ctx.enter_context(nc.Block())

        @block.sync
        def _(sp):
            def row(name, lo, hi):
                return A[name][lo:hi].rearrange("(o n) -> o n", o=1)

            def load_x(batch, t, src):
                sp.dma_start(xs[t % 2], src).then_inc(s[f"x_in{t % 2}"], 16)

            flat = A["x"].rearrange("b s n -> (b s n)")
            flat_out = out.rearrange("b s n -> (b s n)")
            tile_of = lambda a, first: a[bass.ds(first, P * D)].rearrange("(p n) -> p n", n=D)
            xaddr = lambda base, ahead, t: base * (S * D) + (ahead * (S * D) + t * (P * D))

            for t in range(2):
                load_x((0, 0), t, tile_of(flat, xaddr(0, 0, t)))
            sp.dma_start(st_q.rearrange("p (k n) -> p k n", k=KQ),
                         A["Wq"].rearrange("(k p) n -> p k n", p=P)).then_inc(s["wq_in"], 16)
            for i, n in enumerate(("Wk", "Wv")):
                sp.dma_start(st_kv[i].rearrange("p (k n) -> p k n", k=KC),
                             A[n].rearrange("(k p) n -> p k n", p=P)).then_inc(s["wkv_in"], 16)
            sp.dma_start(lut[:, :], row("lut", 0, NLUT).to_broadcast([P, NLUT])).then_inc(s["lut_in"], 16)
            for n, src in (("q", row("bq", 0, D)), ("k", row("bk", 0, D)), ("d", row("bkv_dca", 0, D)), ("o", row("bo", 0, D))):
                sp.dma_start(st_b[n], src.to_broadcast([P, D])).then_inc(s["small_in"], 16)
            sp.dma_start(bvm[:, :], A["bv"]).then_inc(s["small_in"], 16)
            sp.dma_start(bvd[:, :], A["bvd"]).then_inc(s["small_in"], 16)
            for key, name in (("qw", "qn_w"), ("qb", "qn_b"), ("kw", "kn_w"), ("kb", "kn_b")):
                sp.dma_start(lnw[key][:, :], row(name, 0, HD).to_broadcast([P, HD])).then_inc(s["small_in"], 16)
            for key, name in (("kw0", "kn_w"), ("kb0", "kn_b")):
                sp.dma_start(lnw[key][DCA:P, :], row(name, 0, HD).to_broadcast([P - DCA, HD])).then_inc(s["small_in"], 16)
            for key, name in (("kw0", "kn_dca_w"), ("kb0", "kn_dca_b")):
                sp.dma_start(lnw[key][0:DCA, :], row(name, 0, HD).to_broadcast([DCA, HD])).then_inc(s["small_in"], 16)
            sp.dma_start(st_d.rearrange("p (k n) -> p k n", k=KC),
                         A["Wkv_dca"].rearrange("(k p) n -> p k n", p=P)).then_inc(s["wd_in"], 16)
            sp.dma_start(st_o.rearrange("p (k n) -> p k n", k=G),
                         A["Wo"].rearrange("(k p) n -> p k n", p=P)).then_inc(s["wo_in"], 16)
            for c in range(2):
                sp.dma_start(l_idx[c], A["idx"][:, c * CH:(c + 1) * CH]).then_inc(s[f"idx_in{c}"], 16)
            for t in range(2, T):
                sp.wait_ge(s["ps1"], t - 1)
                load_x((0, 0), t, tile_of(flat, xaddr(0, 0, t)))
            sp.wait_ge(s["w_lo"], 5)
            sp.dma_start(ctx_raw.rearrange("p (k n) -> p k n", k=KC),
                         A["ctxT"][0].rearrange("(k p) n -> p k n", p=P)).then_inc(s["ctx_in"], 16)
            for c in range(2, NCH):
                sp.wait_ge(s["mask_set"], c - 1)
                sp.dma_start(l_idx[c % 2], A["idx"][:, c * CH:(c + 1) * CH]).then_inc(s[f"idx_in{c % 2}"], 16)
                if c == NCH - 12:
                    sp.wait_ge(s["hsum_set"], NU)
                    for t in range(2):
                        load_x((0, 1), t, tile_of(flat, xaddr(0, 1, t)))
                if c == NCH - 3:
                    for t in range(2, T):
                        sp.wait_ge(s["ps1"], T + t - 1)
                        load_x((0, 1), t, tile_of(flat, xaddr(0, 1, t)))

            def load_residual(b, first, last):
                if first:
                    sp.wait_ge(s["l_lo"], NCH)
                elif last:
                    sp.wait_ge(s["out_stored"], 16 * T * (B - 1))
                else:
                    sp.wait_ge(s["out_stored"], sp.snap(b * (16 * T)))
                sp.dma_start(x2, A["x"][bass.ds(b, 1)].rearrange("a (t p) n -> p (a t) n", p=P)).then_inc(s["res_in"], 16)

            def store(b, static):
                val = (lambda v: v) if static else sp.snap
                for t in range(T):
                    dst = tile_of(flat_out, val(xaddr(b, 0, t)))
                    sp.wait_ge(s["down_evac"], val(b * (3 * T) + (2 * T + t + 1)))
                    sp.dma_start(dst, x2[:, t, :]).then_inc(s["out_stored"], 16)

            def batch(b, first):
                val = (lambda v: v) if first else sp.snap
                src = [tile_of(flat, val(xaddr(b, 1, t))) for t in range(T)]
                if not first:
                    sp.wait_ge(s["hsum_set"], val(b * NU + NU))
                    load_x((b, 1), 0, src[0])
                    load_x((b, 1), 1, src[1])
                    for t in range(2, T):
                        sp.wait_ge(s["ps1"], val(b * T + (T + t - 1)))
                        load_x((b, 1), t, src[t])
                load_residual(b, first, False)
                sp.wait_ge(s["pv_done"], val(b * (G * T) + G * T))
                sp.dma_start(ctx_raw.rearrange("p (k n) -> p k n", k=KC),
                             A["ctxT"][bass.ds(val(b + 1), 1)].rearrange("a (k p) n -> p (a k) n", p=P)).then_inc(s["ctx_in"], 16)
                store(b, first)

            batch(0, True)
            with sp.Fori(1, B - 1) as b:
                batch(b, False)
            load_residual(B - 1, False, True)
            store(B - 1, True)
            sp.wait_ge(s["out_stored"], 16 * T * B)

        @block.gpsimd
        def _(pool):
            n = [0]
            turns = [0]

            def take_wait():
                turns[0] = turns[0] % 4 + 1
                pool.tensor_tensor(idle[:, turns[0]:turns[0] + 1], mhalf[:, 0:1], mhalf[:, 0:1], ALU.mult)

            def link(ins):
                n[0] += 1
                ins.then_inc(s["pool_chain"], 1)
                pool.wait_ge(s["pool_chain"], n[0])

            pool.memset(mhalf[:, :], -0.5).then_inc(s["ident_set"], 1)
            link(pool.memset(ident[:, :], 0.0))
            pool.affine_select(out=ident[:, :], in_=ident[:, :], compare_op=ALU.not_equal, fill=1.0, base=0,
                               pattern=[[-1, P]], channel_multiplier=1).then_inc(s["ident_set"], 1)
            link(pool.memset(ident_h[:, :], 0.0))
            pool.affine_select(out=ident_h[:, :], in_=ident_h[:, :], compare_op=ALU.not_equal, fill=1.0, base=0,
                               pattern=[[-1, P]], channel_multiplier=1).then_inc(s["ident_set"], 1)
            pool.memset(ones[:, :], 1.0 / 64)
            link(pool.memset(ones_m[:, :], 1.0 / 64))
            link(pool.memset(ones_d[:, :], 0.0))
            pool.memset(ones_m[:, 0:DCA], 0.0)
            pool.memset(ones_d[:, 0:DCA], 1.0 / 64).then_inc(s["ident_set"], 1)
            link(pool.memset(pat[0], 0.0))
            link(pool.memset(pat[1], 0.0))
            for j in range(HALF):
                for i in range(2):
                    link(pool.memset(pat[i][:, j, 4 * j:4 * j + 2], 1.0))
                link(pool.memset(pat[0][0:DCA, j, 4 * j:4 * j + 2], 0.0))
                link(pool.memset(pat[0][0:DCA, j, 4 * j + 2:4 * j + 4], 1.0))
            pool.memset(cmean[:, 0:1], 0.0).then_inc(s["pat_set"], 1)

            def lookup_leaves(c):
                pool.wait_ge(s["b0_set"], c + 1)
                if c:
                    pool.wait_ge(s["l_selected"], c)
                else:
                    pool.wait_ge(s["lut_ready"], 2)
                    pool.wait_ge(s["bias_set"], 4)
                for j in range(4, 8):
                    last = pool.tensor_scalar(l_leaf[j], l_b0[c % 2], lut_d[:, j:j + 1], lut[:, 2 * j:2 * j + 1],
                                              ALU.mult, ALU.add)
                last.then_inc(s["leaf_pool"], 1)

            def lookup_low(c):
                cols = slice(c * CH, (c + 1) * CH)
                pool.wait_ge(s["l_hi"], c + 1)
                pool.tensor_tensor(wf_lo[:, cols], l_w[c % 3], wf_hi[:, cols], ALU.subtract).then_inc(s["l_lo"], 1)

            def ffn(f, piece):
                if piece[0] == "gate_up":
                    it = piece[1]
                    m = rows(it)
                    pool.wait_ge(s["h_set"], nth(f, IT, it + 1))
                    take_wait()
                    pool.tensor_scalar(hT[0][0:m, it % RING, :], sg[it % 2][0:m, :], 1.0, 0.0, ALU.mult, ALU.add)\
                        .then_inc(s["h_hi"], 1)

            def norm(kind, t, bt):
                i = t % 2
                pool.wait_ge(s[f"var{kind}"], nth(bt, T, t + 1))
                pool.tensor_tensor(xrstd[:, kind - 1, i:i + 1], xvar[:, kind - 1, i:i + 1], mhalf[:, 0:1],
                                   ALU.pow).then_inc(s[f"rstd{kind}"], 1)

            def bias(b_):
                if b_ in "kd":
                    pool.wait_ge(s["b_cent"], "kd".index(b_) + 1)
                    take_wait()
                link(pool.tensor_scalar(st_b[b_], st_b[b_], WS, 0.0, ALU.mult, ALU.add))
                take_wait()
                link(pool.tensor_scalar(b16[b_][:, :], st_b[b_], 1.0, 0.0, ALU.mult, ALU.add))
                pool.tensor_tensor(b16[b_][64:P, :], st_b[b_][64:P, :], b16[b_][64:P, :], ALU.subtract).then_inc(s["bias_set"], 1)
                pool.wait_ge(s["bias_set"], "qkdo".index(b_) + 1)

            def split_context(bt):
                pool.wait_ge(s["cT_lo"], nth(bt, 1, 1))
                take_wait()
                for i in range(2):
                    pool.memset(c0["m"][i], 0.0)
                    last = pool.memset(c0["d"][i], 0.0)
                last.then_inc(s["c0_zero"], 1)
                pool.wait_ge(s["c0_zero"], nth(bt, 1, 1))
                take_wait()
                for i in range(2):
                    pool.tensor_scalar(c0["m"][i][:, :, DCA:P], cT[i][:, :, DCA:P], 1.0, 0.0, ALU.mult, ALU.add)
                    last = pool.tensor_scalar(c0["d"][i][:, :, 0:DCA], cT[i][:, :, 0:DCA], 1.0, 0.0, ALU.mult, ALU.add)
                last.then_inc(s["c0_set"], 1)

            def tail(b):
                for t in range(T):
                    norm(2, t, b)

            def core(a, before, between, nxt, prev):
                def rstd(u):
                    pool.wait_ge(s["hvar_set"], nth(a, NU, u + 1))
                    pool.tensor_tensor(hrstd[:, u % 2, :], hvar[:, u % 2, :], mhalf[:, :], ALU.pow).then_inc(s["hrstd_set"], 1)

                def scale(u):
                    w, bb = ((lnw["qw"], lnw["qb"]) if u < T else (lnw["kw0"], lnw["kb0"]) if u == T
                             else (lnw["kw"], lnw["kb"]))
                    v3 = heads(qn[u % 2])
                    pool.wait_ge(s["qc_set"], nth(a, NU, u + 1))
                    pool.tensor_tensor(v3, v3, w[:, :].unsqueeze(1).to_broadcast([P, H, HD]), ALU.mult).then_inc(s["mul_set"], 1)
                    pool.wait_ge(s["mul_set"], nth(a, NU, u + 1))
                    pool.tensor_tensor(v3, v3, bb[:, :].unsqueeze(1).to_broadcast([P, H, HD]), ALU.add).then_inc(s["qn_set"], 1)

                rstd(0)
                if prev is not None:
                    tail(prev)
                else:
                    for b_ in "kdo":
                        bias(b_)
                for u in range(NU + 2):
                    before(u)
                    if u + 1 < NU:
                        rstd(u + 1)
                    if u < NU:
                        scale(u)
                    if u == 0:
                        split_context(a)
                    between(u)
                for slot in range(S_ONE, S_TWO):
                    before(slot)
                    between(slot)
                for n_ in range(G * T):
                    if nxt is not None and n_ in NORM_AT:
                        norm(1, NORM_AT[n_], nxt)
                    before(S_TWO + n_)
                    between(S_TWO + n_)

            for t in range(T):
                norm(1, t, (0, 0))
            nothing = lambda slot: None
            core((0, 0), lambda slot: lookup_leaves(LOOKUP_SLOT[slot]) if slot in LOOKUP_SLOT else None,
                 lambda slot: lookup_low(LOOKUP_SLOT[slot] - 1) if LOOKUP_SLOT.get(slot, 0) else None, (0, 1), None)
            lookup_low(NCH - 1)
            ffn_of = lambda f: lambda slot: ffn(f, FFN_SLOT[slot]) if slot in FFN_SLOT else None
            with pool.Fori(0, B - 2) as b:
                core((b, 1), nothing, ffn_of((b, 0)), (b, 2), (b, 0))
            core((B - 1, 0), nothing, ffn_of((B - 2, 0)), None, (B - 2, 0))
            tail((B - 1, 0))
            for piece in FFN:
                ffn((B - 1, 0), piece)

        @block.scalar
        def _(act):
            def lookup_leaves(c):
                act.wait_ge(s["b0_set"], c + 1)
                if c == 0:
                    act.wait_ge(s["lut_ready"], 2)
                    act.wait_ge(s["bias_set"], 4)
                if c >= 3:
                    act.wait_ge(s["l_lo"], c - 2)
                for j in (0, 1, 3, 2):
                    if c and j:
                        act.wait_ge(s["tree_a" if j == 2 else "pair_a"], c)
                    last = act.activation(l_w[c % 3] if j == 0 else l_leaf[j], l_b0[c % 2], ACT.Identity,
                                          scale=lut_d[:, j:j + 1], bias=lut[:, 2 * j:2 * j + 1])
                last.then_inc(s["leaf_act"], 1)

            def lookup_high(c):
                act.wait_ge(s["l_selected"], c + 1)
                act.activation(wf_hi[:, c * CH:(c + 1) * CH], l_w[c % 3], ACT.Copy).then_inc(s["l_hi"], 1)

            def lookup(c):
                if c:
                    lookup_high(c - 1)
                if c + 1 < NCH:
                    lookup_leaves(c + 1)

            def ffn(f, piece):
                if piece[0] == "gate_up":
                    it = piece[1]
                    m = rows(it)
                    act.wait_ge(s["gate_done"], nth(f, IT, it + 1))
                    if it >= 2:
                        act.wait_ge(s["h_lo"], nth(f, IT, it - 1))
                    act.activation(sg[it % 2][0:m, :], ps[0:m, FB, :], ACT.Tanh, scale=0.5 / WS).then_inc(s["tanh_set"], 1)

            def turn(kind, t, bt):
                act.wait_ge(s[f"ps{kind}"], nth(bt, T, t + 1))
                bank = LB[kind - 1][t]
                act.activation((xT if kind == 1 else xT2)[0][:, :, t * P:(t + 1) * P],
                               ps[:, bank, :].rearrange("p (k s) -> p k s", k=KQ), ACT.Copy).then_inc(s[f"hi{kind}"], 1)

            def context_hi(bt):
                act.wait_ge(s["ctx_in"], nth(bt, 16, 16))
                act.activation(cT[0].rearrange("p k s -> p (k s)"), ctx_raw, ACT.Copy).then_inc(s["cT_hi"], 1)

            def tail(b):
                for t in range(T):
                    turn(2, t, b)

            def square(a, u):
                act.wait_ge(s["proj_done"], nth(a, NU, u + 1))
                if u >= 2:
                    act.wait_ge(s["hsum_set"], nth(a, NU, u - 1))
                act.activation(xs[u % 2], ps[:, AB + u % 2, :], ACT.Square, scale=1.0 / WS).then_inc(s["sq_set"], 1)

            def core(a, between, nxt, prev):
                def values(t):
                    act.wait_ge(s["v_done"], nth(a, T, t + 1))
                    act.activation(v_sb[:, t, :], ps[:, VB + t % 2, :], ACT.Copy, scale=1.0 / WS).then_inc(s["v_evac"], 1)

                def block_hi(u):
                    act.wait_ge(s["qn_set"], nth(a, NU, u + 1))
                    if u >= 2:
                        act.wait_ge(s["blk_ps"], nth(a, 2 * NU, 2 * (u - 1)))
                    src = heads(qn[u % 2])
                    o = blk[u % 2]
                    act.activation(o[:, :, 0:HD], src, ACT.Copy)
                    second = HD if u < T else 2 * HD
                    act.activation(o[:, :, second:second + HD], src, ACT.Copy).then_inc(s["blk_hi"], 1)

                def block_out(u):
                    act.wait_ge(s["blk_ps"], nth(a, 2 * NU, 2 * u + 1))
                    dst = qT if u < T else kT
                    t = u % T
                    act.activation(dst[0:96, 0:HALF, t * P:(t + 1) * P],
                                   ps16(TB)[0:96, :].rearrange("p (h s) -> p h s", h=HALF), ACT.Copy).then_inc(s["blk_act"], 1)

                if prev is not None:
                    square(a, 0)
                    square(a, 1)
                    tail(prev)
                context_hi(a)
                for u in range(NU + 2):
                    if u + 1 < NU:
                        if u:
                            square(a, u + 1)
                        if u + 1 >= T:
                            values(u + 1 - T)
                    if 1 <= u <= NU:
                        block_hi(u - 1)
                    if u >= 2:
                        block_out(u - 2)
                    between(u)

                for m in range(NS):
                    t, p = divmod(m, H // 2)
                    act.wait_ge(s["max_set"], nth(a, NS, m + 1))
                    for j in range(2):
                        h = 2 * p + j
                        sc = ps[:, SC + 2 * (m % 3) + j, DCA:S]
                        last = act.activation(sc, sc, ACT.Exp, bias=nmax[:, 0, t, h:h + 1], accum_out=den[:, 0, t, h:h + 1])
                    last.then_inc(s["S_exp"], 1)
                    between(S_ONE + m)
                act.wait_ge(s["sd_set"], nth(a, 1, 1))
                sdf = sd.rearrange("p r k -> p (r k)")
                act.activation(sdf, sdf, ACT.Exp).then_inc(s["ed_set"], 1)
                act.wait_ge(s["den_set"], nth(a, 1, 1))
                act.wait_ge(s["S_exp"], nth(a, NS, NS))
                dfl = den[:, :, :, :].rearrange("p a t h -> p (a t h)")
                act.activation(dfl, dfl, ACT.Ln).then_inc(s["ln_set"], 1)
                between(S_SHIFT)
                between(S_SHIFT + 1)
                act.wait_ge(s["aug_ps"], nth(a, 1, 1))
                for half in range(2):
                    last = act.activation(qT[96:P, half * HALF, :], ps16(AB)[96:P, half * S:(half + 1) * S], ACT.Copy)
                last.then_inc(s["aug_act"], 1)

                def attn_hi(g):
                    act.wait_ge(s["pv_done"], nth(a, G * T, T * (g + 1)))
                    act.activation(aT[0][g], ps[:, AB + g % 2, :], ACT.Identity, bias=bvs[:, g:g + 1]).then_inc(s["aT_hi"], 1)

                for n_ in range(G * T):
                    for p in range(2):
                        r = 2 * n_ + p
                        act.wait_ge(s["ST_done"], nth(a, NR, r + 1))
                        if p == 0 and n_ >= 2:
                            act.wait_ge(s["pv_done"], nth(a, G * T, n_ - 1))
                        bank = SC + 2 * (r % 2)
                        act.activation(probs[n_ % 2][:, 2 * p:2 * p + 2, :], ps[:, bank:bank + 2, :], ACT.Exp).then_inc(s["probs_set"], 1)
                    if n_ % T == 1 and n_ > T:
                        attn_hi(n_ // T - 1)
                    if nxt is not None and n_ in TURN_AT:
                        turn(1, TURN_AT[n_], nxt)
                    between(S_TWO + n_)
                attn_hi(G - 1)

            fl = lambda a: a[:, :, :].rearrange("p k n -> p (k n)")
            turn(1, 0, (0, 0))
            turn(1, 1, (0, 0))
            act.wait_ge(s["w_cent"], 1)
            act.activation(fl(wq[0]), st_q, ACT.Copy, scale=WS).then_inc(s["w_hi"], 1)
            turn(1, 2, (0, 0))
            turn(1, 3, (0, 0))
            act.wait_ge(s["w_cent"], 2)
            act.activation(fl(wk[0]), st_kv[0], ACT.Copy, scale=WS)
            act.activation(fl(wv[0]), st_kv[1], ACT.Copy, scale=WS).then_inc(s["w_hi"], 1)
            square((0, 0), 0)
            square((0, 0), 1)
            act.wait_ge(s["w_cent"], 3)
            act.activation(fl(wd[0]), st_d, ACT.Copy, scale=WS).then_inc(s["w_hi"], 1)
            act.wait_ge(s["wo_in"], 16)
            act.activation(fl(wo[0]), st_o, ACT.Copy, scale=WS).then_inc(s["w_hi"], 1)
            act.wait_ge(s["pat_ps"], 2)
            for t in range(T):
                for half in range(2):
                    act.activation(kT[96:P, half * HALF:(half + 1) * HALF, t * P:(t + 1) * P],
                                   ps16(TB + min(t, 1))[96:P, :].rearrange("p (h s) -> p h s", h=HALF), ACT.Copy)\
                       .then_inc(s["pat_copied"], 1)
            lookup_leaves(0)
            core((0, 0), lambda slot: lookup(LOOKUP_SLOT[slot]) if slot in LOOKUP_SLOT else None, (0, 1), None)
            lookup_high(NCH - 1)
            ffn_of = lambda f: lambda slot: ffn(f, FFN_SLOT[slot]) if slot in FFN_SLOT else None
            with act.Fori(0, B - 2) as b:
                core((b, 1), ffn_of((b, 0)), (b, 2), (b, 0))
            core((B - 1, 0), ffn_of((B - 2, 0)), None, (B - 2, 0))
            tail((B - 1, 0))
            for piece in FFN:
                ffn((B - 1, 0), piece)

        @block.vector
        def _(dve):
            n = [0]

            def take_wait():
                dve.memset(idle[:, 0:1], 0.0)

            def link(ins):
                n[0] += 1
                ins.then_inc(s["dve_chain"], 1)
                dve.wait_ge(s["dve_chain"], n[0])

            def centre(v):
                r = v.shape[1]
                link(dve.tensor_reduce(cmean[:, 0:r], v, AX_X, ALU.add))
                link(dve.tensor_scalar(cmean[:, 0:r], cmean[:, 0:r], 1.0 / HD, None, ALU.mult))
                return dve.tensor_tensor(v, v, cmean[:, 0:r].unsqueeze(2).to_broadcast([P, r, HD]), ALU.subtract)

            low16 = lambda c: l_idx[c % 2].bitcast(U16).rearrange("p (n e) -> p n e", e=2)[:, :, 0]

            def lookup_bit0(c):
                dve.wait_ge(s[f"idx_in{c % 2}"], 16 * (c // 2 + 1))
                if c >= 2:
                    dve.wait_ge(s["leaf_act"], c - 1)
                    dve.wait_ge(s["leaf_pool"], c - 1)
                dve.tensor_scalar(l_b0[c % 2], low16(c), 1, None, ALU.bitwise_and).then_inc(s["b0_set"], 1)

            def lookup(c):
                if c + 1 < NCH:
                    lookup_bit0(c + 1)
                if c:
                    dve.wait_ge(s["l_selected"], c)
                for i in range(3):
                    last = dve.tensor_scalar(l_m[i], low16(c), 2 << i, None, ALU.bitwise_and)
                last.then_inc(s["mask_set"], 1)
                w = l_w[c % 3]
                L = l_leaf
                dve.wait_ge(s["mask_set"], c + 1)
                dve.wait_ge(s["leaf_act"], c + 1)
                dve.copy_predicated(w, l_m[0], L[1])
                dve.copy_predicated(L[2], l_m[0], L[3]).then_inc(s["pair_a"], 1)
                dve.wait_ge(s["leaf_pool"], c + 1)
                dve.copy_predicated(L[4], l_m[0], L[5])
                dve.copy_predicated(L[6], l_m[0], L[7]).then_inc(s["pair_b"], 1)
                dve.wait_ge(s["pair_a"], c + 1)
                dve.copy_predicated(w, l_m[1], L[2]).then_inc(s["tree_a"], 1)
                dve.wait_ge(s["pair_b"], c + 1)
                dve.copy_predicated(L[4], l_m[1], L[6]).then_inc(s["tree_b"], 1)
                dve.wait_ge(s["tree_a"], c + 1)
                dve.wait_ge(s["tree_b"], c + 1)
                dve.copy_predicated(w, l_m[2], L[4]).then_inc(s["l_selected"], 1)

            def ffn_low(f, it):
                m = rows(it)
                dve.wait_ge(s["h_hi"], nth(f, IT, it + 1))
                dve.tensor_tensor(hT[1][0:m, it % RING, :], sg[it % 2][0:m, :], hT[0][0:m, it % RING, :], ALU.subtract)\
                   .then_inc(s["h_lo"], 1)

            def ffn(f, piece):
                if piece[0] == "gate_up":
                    it = piece[1]
                    m = rows(it)
                    g = sg[it % 2][0:m, :]
                    dve.wait_ge(s["tanh_set"], nth(f, IT, it + 1))
                    dve.scalar_tensor_tensor(out=g, in0=g, scalar=1.0, in1=ps[0:m, FB, :], op0=ALU.add, op1=ALU.mult)\
                       .then_inc(s["gate_used"], 1)
                    dve.wait_ge(s["gate_used"], nth(f, IT, it + 1))
                    dve.wait_ge(s["up_done"], nth(f, IT, it + 1))
                    dve.scalar_tensor_tensor(out=g, in0=g, scalar=0.5 / (WS * WS), in1=ps[0:m, FB + 1, :], op0=ALU.mult,
                                             op1=ALU.mult).then_inc(s["h_set"], 1)
                elif piece[0] == "low":
                    ffn_low(f, piece[1])
                else:
                    _, grp, t0 = piece
                    for t in (t0, t0 + 1):
                        dve.wait_ge(s["down_done"], nth(f, 3 * T, grp * T + t + 1))
                        if grp:
                            dve.wait_ge(s["down_evac"], nth(f, 3 * T, (grp - 1) * T + t + 1))
                        dve.scalar_tensor_tensor(out=x2[:, t, :], in0=ps[:, down_bank(grp, t), :], scalar=1.0 / WS, in1=x2[:, t, :],
                                                 op0=ALU.mult, op1=ALU.add).then_inc(s["down_evac"], 1)

            def norm(kind, t, bt):
                i, kk = t % 2, kind - 1
                src, dst = (xs[i], xs[i]) if kind == 1 else (x2[:, t, :], ln2[t])
                if kind == 1:
                    dve.wait_ge(s[f"x_in{i}"], nth(bt, 8 * T, 16 * (t // 2 + 1)))
                else:
                    dve.wait_ge(s["x2_set"], nth(bt, T, t + 1))
                if t >= 2:
                    dve.wait_ge(s[f"xn{kind}"], nth(bt, T, t - 1))
                dve.bn_stats(stat[:, kk, i, :], src).then_inc(s[f"stat{kind}"], 1)
                dve.wait_ge(s[f"stat{kind}"], nth(bt, T, t + 1))
                take_wait()
                dve.bn_aggr(mv[:, kk, i, :], stat[:, kk, i, :]).then_inc(s[f"mean{kind}"], 1)
                dve.wait_ge(s[f"mean{kind}"], nth(bt, T, t + 1))
                dve.tensor_scalar(xvar[:, kk, i:i + 1], mv[:, kk, i, 1:2], EPS_X, None, ALU.add).then_inc(s[f"var{kind}"], 1)
                dve.wait_ge(s[f"rstd{kind}"], nth(bt, T, t + 1))
                dve.tensor_scalar(dst, src, mv[:, kk, i, 0:1], xrstd[:, kk, i:i + 1], ALU.subtract, ALU.mult)\
                   .then_inc(s[f"xn{kind}"], 1)

            def turn(kind, t, bt):
                dve.wait_ge(s[f"hi{kind}"], nth(bt, T, t + 1))
                cols = slice(t * P, (t + 1) * P)
                x_ = xT if kind == 1 else xT2
                bank = LB[kind - 1][t]
                dve.tensor_tensor(x_[1][:, :, cols], ps[:, bank, :].rearrange("p (k s) -> p k s", k=KQ),
                                  x_[0][:, :, cols], ALU.subtract).then_inc(s[f"lo{kind}"], 1)

            def residual(t, bt):
                dve.wait_ge(s["res_in"], nth(bt, 16, 16))
                dve.wait_ge(s["wo_done"], nth(bt, T, t + 1))
                dve.scalar_tensor_tensor(out=x2[:, t, :], in0=ps[:, VB + t % 2, :], scalar=1.0 / WS, in1=x2[:, t, :],
                                         op0=ALU.mult, op1=ALU.add).then_inc(s["x2_set"], 1)

            def context_lo(bt):
                fc = lambda a_: a_.rearrange("p k s -> p (k s)")
                dve.wait_ge(s["cT_hi"], nth(bt, 1, 1))
                dve.tensor_tensor(fc(cT[1]), ctx_raw, fc(cT[0]), ALU.subtract).then_inc(s["cT_lo"], 1)

            def tail(b):
                for t in range(T):
                    residual(t, b)
                    norm(2, t, b)

            def tail_end(b):
                for t in range(T):
                    turn(2, t, b)

            def variance(a, u):
                i = u % 2
                dve.wait_ge(s["sq_set"], nth(a, NU, u + 1))
                if u >= 2:
                    dve.wait_ge(s["hrstd_set"], nth(a, NU, u - 1))
                dve.tensor_reduce(hvar[:, i, :], heads(xs[i]), AX_X, ALU.add).then_inc(s["hsum_set"], 1)
                dve.wait_ge(s["hsum_set"], nth(a, NU, u + 1))
                dve.tensor_scalar(hvar[:, i, :], hvar[:, i, :], WS * WS / HD, EPS_H * WS * WS, ALU.mult, ALU.add)\
                   .then_inc(s["hvar_set"], 1)

            def normalise(a, u):
                dve.wait_ge(s["hrstd_set"], nth(a, NU, u + 1))
                if u >= 2:
                    dve.wait_ge(s["blk_set"], nth(a, NU, u - 1))
                dve.tensor_tensor(heads(qn[u % 2]), heads(ps[:, AB + u % 2, :]),
                                  hrstd[:, u % 2, :].unsqueeze(2).to_broadcast([P, H, HD]), ALU.mult).then_inc(s["qc_set"], 1)

            def core(a, between, nxt, prev):
                def block_lo(u):
                    dve.wait_ge(s["blk_hi"], nth(a, NU, u + 1))
                    o = blk[u % 2]
                    c_0 = 2 * HD if u < T else HD
                    dve.tensor_tensor(o[:, :, c_0:c_0 + HD], heads(qn[u % 2]), o[:, :, 0:HD], ALU.subtract).then_inc(s["blk_set"], 1)

                def block_out(u):
                    dve.wait_ge(s["blk_ps"], nth(a, 2 * NU, 2 * u + 2))
                    dst = qT if u < T else kT
                    t = u % T
                    dve.tensor_copy(dst[0:96, HALF:H, t * P:(t + 1) * P],
                                    ps16(TB + 1)[0:96, :].rearrange("p (h s) -> p h s", h=HALF)).then_inc(s["blk_dve"], 1)

                if prev is not None:
                    variance(a, 0)
                    tail(prev)
                    variance(a, 1)
                    normalise(a, 0)
                    tail_end(prev)
                for u in range(NU + 2):
                    if 1 <= u < NU:
                        normalise(a, u)
                    if 1 <= u < NU - 1:
                        variance(a, u + 1)
                    if 1 <= u <= NU:
                        block_lo(u - 1)
                    if u >= 2:
                        block_out(u - 2)
                    between(u)
                    if u == 0:
                        context_lo(a)

                for m in range(NS):
                    t, p = divmod(m, H // 2)
                    dve.wait_ge(s["S_done"], nth(a, NS, m + 1))
                    sc = ps[:, SC + 2 * (m % 3):SC + 2 * (m % 3) + 2, :]
                    dve.tensor_reduce(nmax[:, 0, t, 2 * p:2 * p + 2], sc[:, :, DCA:S], AX_X, ALU.max, negate=True)
                    dve.tensor_copy(sd[:, t * H + 2 * p:t * H + 2 * p + 2, :], sc[:, :, 0:DCA]).then_inc(s["max_set"], 1)
                    between(S_ONE + m)
                dve.wait_ge(s["max_set"], nth(a, NS, NS))
                nm1 = nmax[:, 1, :, :].rearrange("p t h -> p (t h)")
                dve.tensor_reduce(nm1, sd, AX_X, ALU.max, negate=True).then_inc(s["dca_max"], 1)
                dve.wait_ge(s["dca_max"], nth(a, 1, 1))
                dve.tensor_tensor(sd, sd, nm1.unsqueeze(2).to_broadcast([P, T * H, DCA]), ALU.add).then_inc(s["sd_set"], 1)
                dve.wait_ge(s["ed_set"], nth(a, 1, 1))
                dve.tensor_reduce(den[:, 1, :, :].rearrange("p t h -> p (t h)"), sd, AX_X, ALU.add).then_inc(s["den_set"], 1)
                between(S_SHIFT)
                dve.wait_ge(s["ln_set"], nth(a, 1, 1))
                fs = lambda a_: a_[:, :, :, :].rearrange("p a t h -> p (a t h)")
                dve.tensor_tensor(fs(shift), fs(nmax), fs(den), ALU.subtract).then_inc(s["shift_set"], 1)
                dve.wait_ge(s["shift_set"], nth(a, 1, 1))
                for w in range(2):
                    last = dve.tensor_copy(caug[:, :, :, w, 0], shift[:, w, :, :])
                last.then_inc(s["c_hi"], 1)
                dve.wait_ge(s["c_hi"], nth(a, 1, 1))
                for w in range(2):
                    last = dve.tensor_tensor(caug[:, :, :, w, 1], shift[:, w, :, :], caug[:, :, :, w, 0], ALU.subtract)
                last.then_inc(s["c_set"], 1)
                between(S_SHIFT + 1)
                dve.wait_ge(s["aug_act"], nth(a, 1, 1))
                for h0, lo, hi in AUG:
                    dve.tensor_copy(qT[96:P, lo:hi, :], qT[96:P, h0:h0 + 1, :].to_broadcast([32, hi - lo, S])).then_inc(s["aug_dve"], 1)

                def attn_lo(g):
                    dve.wait_ge(s["aT_hi"], nth(a, G, g + 1))
                    dve.scalar_tensor_tensor(out=aT[1][g], in0=ps[:, AB + g % 2, :], scalar=bvs[:, g:g + 1], in1=aT[0][g],
                                             op0=ALU.add, op1=ALU.subtract).then_inc(s["aT_lo"], 1)

                for n_ in range(G * T):
                    if n_ % T == 1 and n_ > T:
                        attn_lo(n_ // T - 1)
                    if nxt is not None:
                        if n_ in NORM_AT:
                            norm(1, NORM_AT[n_], nxt)
                        if n_ in TURN_AT:
                            turn(1, TURN_AT[n_], nxt)
                    between(S_TWO + n_)
                attn_lo(G - 1)

            fl = lambda a: a[:, :, :].rearrange("p k n -> p (k n)")

            def low(dst, src, hi):
                return dve.scalar_tensor_tensor(out=dst, in0=src, scalar=WS, in1=hi, op0=ALU.mult, op1=ALU.subtract)

            def bias(b_):
                link(dve.tensor_scalar(st_b[b_], st_b[b_], WS, None, ALU.mult))
                link(dve.tensor_scalar(b16[b_][:, :], st_b[b_], 1.0, None, ALU.mult))
                dve.tensor_tensor(b16[b_][64:P, :], st_b[b_][64:P, :], b16[b_][64:P, :], ALU.subtract).then_inc(s["bias_set"], 1)

            dve.wait_ge(s["pat_set"], 1)
            norm(1, 0, (0, 0))
            norm(1, 1, (0, 0))
            dve.wait_ge(s["wq_in"], 16)
            centre(heads(st_q)).then_inc(s["w_cent"], 1)
            n_small = 4 + 2 + 4 + 2 + 2
            dve.wait_ge(s["small_in"], 16 * n_small)
            dve.wait_ge(s["w_cent"], 1)
            link(centre(heads(st_b["q"])))
            bias("q")
            turn(1, 0, (0, 0))
            turn(1, 1, (0, 0))
            dve.wait_ge(s["w_hi"], 1)
            low(fl(wq[1]), st_q, fl(wq[0])).then_inc(s["w_lo"], 1)
            norm(1, 2, (0, 0))
            norm(1, 3, (0, 0))
            turn(1, 2, (0, 0))
            turn(1, 3, (0, 0))
            dve.wait_ge(s["wkv_in"], 32)
            centre(heads(st_kv[0])).then_inc(s["w_cent"], 1)
            dve.wait_ge(s["wd_in"], 16)
            dk = st_d.rearrange("p (k n) -> p k n", k=KC)
            dve.wait_ge(s["w_cent"], 2)
            link(centre(heads(dk[:, 0, 0:D])))
            centre(heads(dk[:, 1, 0:D])).then_inc(s["w_cent"], 1)
            dve.wait_ge(s["w_cent"], 3)
            for b_ in "kd":
                last = centre(heads(st_b[b_]))
                last.then_inc(s["b_cent"], 1)
                dve.wait_ge(s["b_cent"], "kd".index(b_) + 1)
            dve.tensor_scalar(lnw["qw"][:, :], lnw["qw"][:, :], QK_SCALE, None, ALU.mult)
            dve.tensor_scalar(lnw["qb"][:, :], lnw["qb"][:, :], QK_SCALE, None, ALU.mult)
            link(dve.tensor_tensor(bvs[:, :], bvm[:, :], bvd[:, :], ALU.add))
            dve.wait_ge(s["lut_in"], 16)
            link(dve.tensor_scalar(lut[:, :], lut[:, :], WS, None, ALU.mult))
            lp = lut[:, :].rearrange("p (j e) -> p j e", e=2)
            dve.tensor_tensor(lut_d[:, :], lp[:, :, 1], lp[:, :, 0], ALU.subtract).then_inc(s["lut_ready"], 2)
            variance((0, 0), 0)
            dve.wait_ge(s["w_hi"], 2)
            low(fl(wk[1]), st_kv[0], fl(wk[0])).then_inc(s["w_lo"], 1)
            low(fl(wv[1]), st_kv[1], fl(wv[0])).then_inc(s["w_lo"], 1)
            normalise((0, 0), 0)
            dve.wait_ge(s["w_hi"], 3)
            low(fl(wd[1]), st_d, fl(wd[0])).then_inc(s["w_lo"], 1)
            dve.wait_ge(s["w_hi"], 4)
            low(fl(wo[1]), st_o, fl(wo[0])).then_inc(s["w_lo"], 1)
            variance((0, 0), 1)
            lookup_bit0(0)
            core((0, 0), lambda slot: lookup(LOOKUP_SLOT[slot]) if slot in LOOKUP_SLOT else None, (0, 1), None)
            ffn_of = lambda f: lambda slot: ffn(f, FFN_SLOT[slot]) if slot in FFN_SLOT else None
            with dve.Fori(0, B - 2) as b:
                core((b, 1), ffn_of((b, 0)), (b, 2), (b, 0))
            core((B - 1, 0), ffn_of((B - 2, 0)), None, (B - 2, 0))
            tail((B - 1, 0))
            tail_end((B - 1, 0))
            for piece in FFN:
                ffn((B - 1, 0), piece)

        @block.tensor
        def _(pe):
            pe.wait_ge(s["pat_set"], 1)
            pe.wait_ge(s["ident_set"], 4)
            for i in range(2):
                for j in range(HALF):
                    last = pe.transpose(ps16(TB + i)[96:P, j * P:(j + 1) * P], pat[i][:, j, :], ident_h[:, :])
                last.then_inc(s["pat_ps"], 1)

            def product(dst, terms, wait=None):
                todo = []
                for lhs, rhs in terms:
                    if isinstance(lhs, list):
                        todo += [(lhs[0], rhs[0]), (lhs[0], rhs[1]), (lhs[1], rhs[0])]
                    else:
                        todo.append((lhs, rhs))
                for i, (l, r) in enumerate(todo):
                    last = pe.matmul(dst, l, r, start=(i == 0), stop=(i == len(todo) - 1))
                return last

            both = lambda f: [f(0), f(1)]

            def ffn(f, piece):
                wf = (wf_hi, wf_lo)
                if piece[0] == "gate_up":
                    it = piece[1]
                    m = rows(it)
                    if it == 0:
                        pe.wait_ge(s["lo2"], nth(f, T, T))
                    if it in (5, 9):
                        pe.wait_ge(s["down_evac"], nth(f, 3 * T, T * (1 if it == 5 else 2)))
                    for o, c_0, used, done in ((0, 0, "gate_used", "gate_done"), (1, UP0, "h_set", "up_done")):
                        if it:
                            pe.wait_ge(s[used], nth(f, IT, it))
                        product(ps[0:m, FB + o, :],
                                [(both(lambda a_: wf[a_][:, c_0 + i * INTER + it * P:c_0 + i * INTER + it * P + m]),
                                  both(lambda a_: xT2[a_][:, i, :])) for i in range(KQ)]).then_inc(s[done], 1)
                elif piece[0] == "down":
                    _, grp, t0 = piece
                    lo, hi = DOWN[grp]
                    if t0 == 0:
                        pe.wait_ge(s["h_lo"], nth(f, IT, hi))
                        pe.wait_ge(s["h_set"], nth(f, IT, (5, 9, IT)[grp]))
                    for t in (t0, t0 + 1):
                        if t >= 2 and grp < 2:
                            pe.wait_ge(s["down_evac"], nth(f, 3 * T, grp * T + t - 1))
                        product(ps[:, down_bank(grp, t), :],
                                [(both(lambda a_: hT[a_][0:rows(i), i % RING, t * P:(t + 1) * P]),
                                  both(lambda a_: wf[a_][0:rows(i), DN0 + i * D:DN0 + (i + 1) * D])) for i in range(lo, hi)])\
                            .then_inc(s["down_done"], 1)

            def turn(kind, t, bt):
                src = xs[t % 2] if kind == 1 else ln2[t]
                bank = LB[kind - 1][t]
                pe.wait_ge(s[f"xn{kind}"], nth(bt, T, t + 1))
                if t >= 2 and kind == 1:
                    pe.wait_ge(s["lo1"], nth(bt, T, t - 1))
                for k in range(KQ):
                    last = pe.transpose(ps[:, bank, k * P:(k + 1) * P], src[:, k * P:(k + 1) * P], ident[:, :])
                last.then_inc(s[f"ps{kind}"], 1)

            def tail(b):
                pe.wait_ge(s["aT_lo"], nth(b, G, G))
                for t in range(T):
                    if t >= 2:
                        pe.wait_ge(s["x2_set"], nth(b, T, t - 1))
                    product(ps[:, VB + t % 2, :],
                            [(both(lambda a_: aT[a_][g][:, t * P:(t + 1) * P]), both(lambda a_: wo[a_][:, g, :])) for g in range(G)]
                            + [(ones[:, :], b16["o"][:, :])]).then_inc(s["wo_done"], 1)

            def tail_end(b):
                for t in range(T):
                    turn(2, t, b)

            def core(a, between, nxt, prev):
                def project(u):
                    t = u % T
                    cols = slice(t * P, (t + 1) * P)
                    if u >= 2:
                        pe.wait_ge(s["qc_set"], nth(a, NU, u - 1))
                    elif prev is not None:
                        pe.wait_ge(s["aT_lo"], nth(prev, G, G - 1 + u))
                    if u < T:
                        pe.wait_ge(s["lo1"], nth(a, T, t + 1))
                        product(ps[:, AB + u % 2, :],
                                [(both(lambda a_: xT[a_][:, i, cols]), both(lambda a_: wq[a_][:, i, :])) for i in range(KQ)]
                                + [(ones[:, :], b16["q"][:, :])]).then_inc(s["proj_done"], 1)
                        return
                    if t == 0:
                        pe.wait_ge(s["c0_set"], nth(a, 1, 1))
                        main, dca = c0["m"], c0["d"]
                        keys = [(both(lambda a_: main[a_][:, i, :]), both(lambda a_: wk[a_][:, i, :])) for i in range(KC)]
                        keys += [(both(lambda a_: dca[a_][:, i, :]), both(lambda a_: wd[a_][:, i, 0:D])) for i in range(KC)]
                        keys += [(ones_m[:, :], b16["k"][:, :]), (ones_d[:, :], b16["d"][:, :])]
                        vals = [(both(lambda a_: main[a_][:, i, :]), both(lambda a_: wv[a_][:, i, :])) for i in range(KC)]
                        vals += [(both(lambda a_: dca[a_][:, i, :]), both(lambda a_: wd[a_][:, i, D:2 * D])) for i in range(KC)]
                    else:
                        keys = [(both(lambda a_: cT[a_][:, i, cols]), both(lambda a_: wk[a_][:, i, :])) for i in range(KC)]
                        keys += [(ones[:, :], b16["k"][:, :])]
                        vals = [(both(lambda a_: cT[a_][:, i, cols]), both(lambda a_: wv[a_][:, i, :])) for i in range(KC)]
                    product(ps[:, AB + u % 2, :], keys).then_inc(s["proj_done"], 1)
                    if t >= 2:
                        pe.wait_ge(s["v_evac"], nth(a, T, t - 1))
                    product(ps[:, VB + t % 2, :], vals).then_inc(s["v_done"], 1)

                def transpose_blocks(u):
                    pe.wait_ge(s["blk_set"], nth(a, NU, u + 1))
                    for half in range(2):
                        if u:
                            pe.wait_ge(s["blk_act" if half == 0 else "blk_dve"], nth(a, NU, u))
                        for j in range(HALF):
                            last = pe.transpose(ps16(TB + half)[0:96, j * P:(j + 1) * P], blk[u % 2][:, half * HALF + j, :], ident_h[:, :])
                        last.then_inc(s["blk_ps"], 1)

                project(0)
                if prev is not None:
                    tail(prev)
                project(1)
                if prev is not None:
                    tail_end(prev)
                for u in range(NU + 2):
                    if 1 <= u < NU - 1:
                        project(u + 1)
                    if u >= 2:
                        transpose_blocks(u - 2)
                    between(u)

                pe.wait_ge(s["blk_act"], nth(a, NU, NU))
                pe.wait_ge(s["blk_dve"], nth(a, NU, NU))
                pe.wait_ge(s["v_evac"], nth(a, T, T))
                for m in range(NS):
                    t, p = divmod(m, H // 2)
                    if m >= 3:
                        pe.wait_ge(s["S_exp"], nth(a, NS, m - 2))
                    for j in range(2):
                        h = 2 * p + j
                        last = pe.matmul(ps[:, SC + 2 * (m % 3) + j, :], qT[0:96, h, t * P:(t + 1) * P], kT[0:96, h, :], start=True, stop=True)
                    last.then_inc(s["S_done"], 1)
                    between(S_ONE + m)
                between(S_SHIFT)
                pe.wait_ge(s["S_exp"], nth(a, NS, NS))
                between(S_SHIFT + 1)
                pe.wait_ge(s["c_set"], nth(a, 1, 1))
                for half in range(2):
                    for t in range(T):
                        last = pe.transpose(ps16(AB)[96:P, half * S + t * P:half * S + (t + 1) * P],
                                            caug[:, t, half * HALF:(half + 1) * HALF].rearrange("p h a c -> p (h a c)"), ident_h[:, :])
                last.then_inc(s["aug_ps"], 1)
                if prev is not None:
                    pe.wait_ge(s["down_evac"], nth(prev, 3 * T, 3 * T))

                def scores_t(n_):
                    g, kt = divmod(n_, T)
                    if kt == 0 and g < len(AUG):
                        pe.wait_ge(s["aug_dve"], nth(a, len(AUG), g + 1))
                    for p in range(2):
                        r = 2 * n_ + p
                        if r >= 2:
                            pe.wait_ge(s["probs_set"], nth(a, NR, r - 1))
                        for j in range(2):
                            h = g * HG + 2 * p + j
                            last = pe.matmul(ps[:, SC + 2 * (r % 2) + j, :], kT[:, h, kt * P:(kt + 1) * P], qT[:, h, :], start=True, stop=True)
                        last.then_inc(s["ST_done"], 1)

                def weigh_values(n_):
                    g, kt = divmod(n_, T)
                    pe.wait_ge(s["probs_set"], nth(a, NR, 2 * n_ + 2))
                    if kt == 0 and g >= 2:
                        pe.wait_ge(s["aT_lo"], nth(a, G, g - 1))
                    for j in range(HG):
                        h = g * HG + j
                        last = pe.matmul(ps[j * HD:(j + 1) * HD, AB + g % 2, :], v_sb[:, kt, h * HD:(h + 1) * HD], probs[n_ % 2][:, j, :],
                                         start=(kt == 0), stop=(kt == T - 1), tile_position=(0, j * HD))
                    last.then_inc(s["pv_done"], 1)

                for n_ in range(G * T + 1):
                    if n_ < G * T:
                        scores_t(n_)
                    if n_:
                        weigh_values(n_ - 1)
                    if nxt is not None and n_ in TURN_AT:
                        turn(1, TURN_AT[n_], nxt)
                    if n_ < G * T:
                        between(S_TWO + n_)

            for t in range(T):
                turn(1, t, (0, 0))
            pe.wait_ge(s["w_lo"], 1)
            pe.wait_ge(s["bias_set"], 1)
            core((0, 0), lambda slot: None, (0, 1), None)
            pe.wait_ge(s["l_lo"], NCH)
            ffn_of = lambda f: lambda slot: ffn(f, FFN_SLOT[slot]) if slot in FFN_SLOT else None
            with pe.Fori(0, B - 2) as b:
                core((b, 1), ffn_of((b, 0)), (b, 2), (b, 0))
            core((B - 1, 0), ffn_of((B - 2, 0)), None, (B - 2, 0))
            tail((B - 1, 0))
            tail_end((B - 1, 0))
            for piece in FFN:
                ffn((B - 1, 0), piece)


def kernel(**inputs):
    import numpy as np
    import concourse.bacc as bacc
    from concourse.bass_utils import run_bass_kernel_spmd

    nc = bacc.Bacc("TRN2", target_bir_lowering=False, num_devices=1)
    src = {k.replace("L0_xattn_", "").replace("L0_ffn_", ""): np.asarray(v) for k, v in inputs.items()}
    arrays, args = {}, {}

    def give(name, a):
        a = np.ascontiguousarray(a)
        arrays[f"in_{name}"] = a
        args[name] = nc.dram_tensor(f"in_{name}", a.shape, mybir.dt.from_np(a.dtype), kind="ExternalInput").ap()

    for name in ("x", "Wq", "bq", "Wkv_dca", "bkv_dca", "qn_w", "qn_b", "kn_w", "kn_b", "kn_dca_w", "kn_dca_b", "Wo", "bo", "lut"):
        give(name, src[name])
    w = np.concatenate([src["Wk"], src["Wv"]], axis=1).reshape(KD, H, 2, HD)
    give("Wk", w[:, :, 0].reshape(KD, D))
    give("Wv", w[:, :, 1].reshape(KD, D))
    bias = np.concatenate([src["bk"], src["bv"]]).reshape(H, 2, HD)
    give("bk", bias[:, 0].reshape(D))
    give("bv", bias[:, 1].reshape(G, P).T)
    give("bvd", src["bkv_dca"][D:].reshape(G, P).T)
    c = src["ctx_1024"]
    give("ctxT", np.concatenate([c[:, S - DCA:], c[:, :S - DCA]], axis=1).transpose(0, 2, 1))
    gate = src["gate_idx"].T.reshape(KQ, P, INTER).transpose(1, 0, 2).reshape(P, KQ * INTER)
    up = src["up_idx"].T.reshape(KQ, P, INTER).transpose(1, 0, 2).reshape(P, KQ * INTER)
    down = np.pad(src["down_idx"].T, ((0, IT * P - INTER), (0, 0))).reshape(IT, P, D).transpose(1, 0, 2).reshape(P, IT * D)
    give("idx", np.concatenate([gate, up, down], axis=1))
    out = nc.dram_tensor("out", (B, S, D), F32, kind="ExternalOutput").ap()
    xattn_ffn(nc, args, out)
    r = run_bass_kernel_spmd(nc, [arrays], core_ids=[0])
    return r.results[0]["out"]
```
